# Optimizing a Trainium2 kernel written in Bass

```python
import numpy as np
import jax
import jax.numpy as jnp

def _softmax(x, axis=-1):
    return jax.nn.softmax(x, axis=axis)

def _gelu(x):
    return jax.nn.gelu(x, approximate=True)

def _silu(x):
    return jax.nn.silu(x)

def _sigmoid(x):
    return jax.nn.sigmoid(x)

def _layernorm(x, axis=-1, eps=1e-05):
    m = jnp.mean(x, axis=axis, keepdims=True)
    v = jnp.var(x, axis=axis, keepdims=True)
    return (x - m) / jnp.sqrt(v + eps)

def _scatter_add(tgt, idx, src, axis=0):
    return tgt.at[idx].add(src)

def _segment_sum(src, seg, n):
    return jax.ops.segment_sum(src, seg, n)
kernel_name = 'mk_decoder_preln_d1_seqx_r8_1adec1'

def setup_inputs(seed: int=0):
    np.random.seed(seed)
    _w = jnp.asarray

    def _rec_inputs():
        import jax
        import jax.numpy as jnp
        _rk = jax.random.key(seed)
        x = -0.0002928 + 1 * jax.random.normal(jax.random.fold_in(_rk, 1), (16, 100, 128), jnp.float32)
        _lenS = 100 - jax.random.randint(jax.random.fold_in(_rk, 7), (16,), 0, max(1, 100 // 4) + 1, jnp.int32)
        _lenS2 = 1444 - jax.random.randint(jax.random.fold_in(_rk, 8), (16,), 0, max(1, 1444 // 4) + 1, jnp.int32)
        _ctx_1024P = jax.random.normal(jax.random.fold_in(_rk, 11), (16, 16, 128), jnp.float32)
        _ctx_1024c = jax.random.dirichlet(jax.random.fold_in(_rk, 511), 0.3 * jnp.ones((16,), jnp.float32), (16, 1444))
        _ctx_1024t = jnp.einsum('bsk,bkd->bsd', _ctx_1024c, _ctx_1024P)
        _ctx_1024t = _ctx_1024t * jax.lax.rsqrt(jnp.mean(jnp.square(_ctx_1024t)) + 1e-12) * 0.953939
        ctx_1024 = -1.39393e-06 + 0.999914 * (_ctx_1024t + 0.3 * jax.random.normal(jax.random.fold_in(_rk, 611), (16, 1444, 128), jnp.float32))
        _validS = jnp.arange(100)[None, :] < _lenS[:, None]
        _validS2 = jnp.arange(1444)[None, :] < _lenS2[:, None]
        _causal = jnp.tril(jnp.ones((100, 100), dtype=bool))
        mask_BxSxS2_bk1 = jnp.broadcast_to(_validS2[:, None, :], (16, 100, 1444))
        return (x, ctx_1024, mask_BxSxS2_bk1)
    x, ctx_1024, mask_BxSxS2_bk1 = _rec_inputs()

    def _L0_attn_setup():
        import jax, jax.numpy as jnp
        import numpy as np
        ATT_WIDTH = 64

        def _band_mask(T, width, dtype):
            lower = width // 2
            upper = (width - 1) // 2
            i = jnp.arange(T)[:, None]
            j = jnp.arange(T)[None, :]
            keep = (i - j <= lower) & (j - i <= upper)
            return keep.astype(dtype)
        key = jax.random.key(seed)
        k1, k2, k3, k4 = jax.random.split(key, 4)
        B, T, H, D = (8, 256, 128, 128)
        scale = 1.0 / np.sqrt(H)
        return {'inputs': jax.random.normal(k1, (B, T, H), dtype=jnp.float32), 'WQ': jax.random.normal(k2, (H, D), dtype=jnp.float32) * scale, 'WK': jax.random.normal(k3, (H, D), dtype=jnp.float32) * scale, 'WV': jax.random.normal(k4, (H, D), dtype=jnp.float32) * scale}
    _L0_attn_all = _L0_attn_setup()
    _L0_attn_in = {k: v for k, v in _L0_attn_all.items() if k in ('WQ', 'WK', 'WV')}
    del _L0_attn_all

    def _L0_xattn_setup():
        import jax, jax.numpy as jnp
        import numpy as np
        D_MODEL = 128
        NUM_HEADS = 16
        D_K = 64
        D_V = 64
        B, L = (2, 256)
        key = jax.random.key(seed)
        ks = jax.random.split(key, 12)
        std_qk = np.sqrt(2.0 / (D_MODEL + D_K)).astype(np.float32)
        std_v = np.sqrt(2.0 / (D_MODEL + D_V)).astype(np.float32)
        return {'input_Q': jax.random.normal(ks[0], (B, L, D_MODEL), jnp.float32), 'input_K': jax.random.normal(ks[1], (B, L, D_MODEL), jnp.float32), 'input_V': jax.random.normal(ks[2], (B, L, D_MODEL), jnp.float32), 'attn_mask': jax.random.randint(ks[3], (B, L, L), 0, 2).astype(jnp.bool_), 'W_Q': std_qk * jax.random.normal(ks[4], (NUM_HEADS * D_K, D_MODEL), jnp.float32), 'b_Q': jnp.zeros((NUM_HEADS * D_K,), jnp.float32), 'W_K': std_qk * jax.random.normal(ks[5], (NUM_HEADS * D_K, D_MODEL), jnp.float32), 'b_K': jnp.zeros((NUM_HEADS * D_K,), jnp.float32), 'W_V': std_v * jax.random.normal(ks[6], (NUM_HEADS * D_V, D_MODEL), jnp.float32), 'b_V': jnp.zeros((NUM_HEADS * D_V,), jnp.float32), 'W_out': std_v * jax.random.normal(ks[7], (D_MODEL, NUM_HEADS * D_V), jnp.float32), 'b_out': jnp.zeros((D_MODEL,), jnp.float32)}
    _L0_xattn_all = _L0_xattn_setup()
    _L0_xattn_in = {k: v for k, v in _L0_xattn_all.items() if k in ('W_Q', 'b_Q', 'W_K', 'b_K', 'W_V', 'b_V', 'W_out', 'b_out')}
    del _L0_xattn_all

    def _L0_ffn_setup():
        import jax, jax.numpy as jnp
        import numpy as np
        B, T, D = (2, 128, 128)
        E = 16
        H = 256
        K = 2
        HS = H * 2
        key = jax.random.key(seed)
        ks = jax.random.split(key, 16)
        s = 0.02
        f32 = jnp.float32
        return {'x': jax.random.normal(ks[0], (B, T, D), f32), 'Wg': jax.random.normal(ks[1], (D, E), f32) * s, 'W1': jax.random.normal(ks[2], (E, D, H), f32) * s, 'b1': jax.random.normal(ks[3], (E, H), f32) * s, 'W11': jax.random.normal(ks[4], (E, D, H), f32) * s, 'b11': jax.random.normal(ks[5], (E, H), f32) * s, 'W2': jax.random.normal(ks[6], (E, H, D), f32) * s, 'b2': jax.random.normal(ks[7], (E, D), f32) * s, 'Ws1': jax.random.normal(ks[8], (D, HS), f32) * s, 'bs1': jax.random.normal(ks[9], (HS,), f32) * s, 'Ws11': jax.random.normal(ks[10], (D, HS), f32) * s, 'bs11': jax.random.normal(ks[11], (HS,), f32) * s, 'Ws2': jax.random.normal(ks[12], (HS, D), f32) * s, 'bs2': jax.random.normal(ks[13], (D,), f32) * s}
    _L0_ffn_all = _L0_ffn_setup()
    _L0_ffn_in = {k: v for k, v in _L0_ffn_all.items() if k in ('Wg', 'W1', 'b1', 'W11', 'b11', 'W2', 'b2', 'Ws1', 'bs1', 'Ws11', 'bs11', 'Ws2', 'bs2')}
    del _L0_ffn_all
    return {'x': x, 'ctx_1024': ctx_1024, 'mask_BxSxS2_bk1': mask_BxSxS2_bk1, 'L0_attn_WQ': _L0_attn_in['WQ'], 'L0_attn_WK': _L0_attn_in['WK'], 'L0_attn_WV': _L0_attn_in['WV'], 'L0_xattn_W_Q': _L0_xattn_in['W_Q'], 'L0_xattn_b_Q': _L0_xattn_in['b_Q'], 'L0_xattn_W_K': _L0_xattn_in['W_K'], 'L0_xattn_b_K': _L0_xattn_in['b_K'], 'L0_xattn_W_V': _L0_xattn_in['W_V'], 'L0_xattn_b_V': _L0_xattn_in['b_V'], 'L0_xattn_W_out': _L0_xattn_in['W_out'], 'L0_xattn_b_out': _L0_xattn_in['b_out'], 'L0_ffn_Wg': _L0_ffn_in['Wg'], 'L0_ffn_W1': _L0_ffn_in['W1'], 'L0_ffn_b1': _L0_ffn_in['b1'], 'L0_ffn_W11': _L0_ffn_in['W11'], 'L0_ffn_b11': _L0_ffn_in['b11'], 'L0_ffn_W2': _L0_ffn_in['W2'], 'L0_ffn_b2': _L0_ffn_in['b2'], 'L0_ffn_Ws1': _L0_ffn_in['Ws1'], 'L0_ffn_bs1': _L0_ffn_in['bs1'], 'L0_ffn_Ws11': _L0_ffn_in['Ws11'], 'L0_ffn_bs11': _L0_ffn_in['bs11'], 'L0_ffn_Ws2': _L0_ffn_in['Ws2'], 'L0_ffn_bs2': _L0_ffn_in['bs2']}

def reference(x, ctx_1024, mask_BxSxS2_bk1, L0_attn_WQ, L0_attn_WK, L0_attn_WV, L0_xattn_W_Q, L0_xattn_b_Q, L0_xattn_W_K, L0_xattn_b_K, L0_xattn_W_V, L0_xattn_b_V, L0_xattn_W_out, L0_xattn_b_out, L0_ffn_Wg, L0_ffn_W1, L0_ffn_b1, L0_ffn_W11, L0_ffn_b11, L0_ffn_W2, L0_ffn_b2, L0_ffn_Ws1, L0_ffn_bs1, L0_ffn_Ws11, L0_ffn_bs11, L0_ffn_Ws2, L0_ffn_bs2):
    import jax
    import jax.numpy as jnp

    def _L0_attn_ref(inputs, WQ, WK, WV):
        import jax, jax.numpy as jnp
        import numpy as np
        ATT_WIDTH = 64

        def _band_mask(T, width, dtype):
            lower = width // 2
            upper = (width - 1) // 2
            i = jnp.arange(T)[:, None]
            j = jnp.arange(T)[None, :]
            keep = (i - j <= lower) & (j - i <= upper)
            return keep.astype(dtype)
        B, T, H = inputs.shape
        D = WQ.shape[1]
        scale = jnp.asarray(D, inputs.dtype) ** 0.5
        q = jnp.einsum('bth,hd->btd', inputs, WQ)
        k = jnp.einsum('bth,hd->btd', inputs, WK)
        v = jnp.einsum('bth,hd->btd', inputs, WV)
        score = jnp.einsum('bqd,bkd->bqk', q, k) / scale
        local = _band_mask(T, ATT_WIDTH, score.dtype)
        score = score * local[None, :, :]
        attn = jax.nn.softmax(score, axis=-1)
        return jnp.einsum('bqk,bkd->bqd', attn, v)

    def _L0_xattn_ref(input_Q, input_K, input_V, attn_mask, W_Q, b_Q, W_K, b_K, W_V, b_V, W_out, b_out):
        import jax, jax.numpy as jnp
        import numpy as np
        D_MODEL = 128
        NUM_HEADS = 16
        D_K = 64
        D_V = 64
        B, L = (2, 256)
        batch = input_Q.shape[0]
        Q = (input_Q @ W_Q.T + b_Q).reshape(batch, -1, NUM_HEADS, D_K).transpose(0, 2, 1, 3)
        K = (input_K @ W_K.T + b_K).reshape(batch, -1, NUM_HEADS, D_K).transpose(0, 2, 1, 3)
        V = (input_V @ W_V.T + b_V).reshape(batch, -1, NUM_HEADS, D_V).transpose(0, 2, 1, 3)
        scores = jnp.einsum('bhqd,bhkd->bhqk', Q, K) / np.sqrt(D_K).astype(np.float32)
        scores = jnp.where(attn_mask[:, None, :, :], jnp.float32(-10000.0), scores)
        attn = jax.nn.softmax(scores, axis=-1)
        out = jnp.einsum('bhqk,bhkd->bhqd', attn, V)
        out = out.transpose(0, 2, 1, 3).reshape(batch, -1, NUM_HEADS * D_V)
        return out @ W_out.T + b_out

    def _L0_ffn_ref(x, Wg, W1, b1, W11, b11, W2, b2, Ws1, bs1, Ws11, bs11, Ws2, bs2):
        import jax, jax.numpy as jnp
        import numpy as np
        B, T, D = (2, 128, 128)
        E = 16
        H = 256
        K = 2
        HS = H * 2
        b, t, d = x.shape
        xf = x.reshape(b * t, d)
        n = xf.shape[0]
        logits = xf @ Wg
        _, topi = jax.lax.top_k(logits, K)
        mask = jnp.zeros((n, E), bool).at[jnp.arange(n)[:, None], topi].set(True)
        gates = jax.nn.softmax(jnp.where(mask, logits, -jnp.inf), axis=-1)
        y = jnp.zeros_like(xf)
        for e in range(E):
            h = jax.nn.silu(xf @ W1[e] + b1[e]) * (xf @ W11[e] + b11[e])
            y = y + (h @ W2[e] + b2[e]) * gates[:, e, None]
        z = jax.nn.silu(xf @ Ws1 + bs1) * (xf @ Ws11 + bs11) @ Ws2 + bs2
        return (y + z).reshape(b, t, d)
    x = x + _L0_attn_ref(_layernorm(x, axis=-1), L0_attn_WQ, L0_attn_WK, L0_attn_WV)
    x = x + _L0_xattn_ref(_layernorm(x, axis=-1), ctx_1024, ctx_1024, mask_BxSxS2_bk1, L0_xattn_W_Q, L0_xattn_b_Q, L0_xattn_W_K, L0_xattn_b_K, L0_xattn_W_V, L0_xattn_b_V, L0_xattn_W_out, L0_xattn_b_out)
    x = x + _L0_ffn_ref(_layernorm(x, axis=-1), L0_ffn_Wg, L0_ffn_W1, L0_ffn_b1, L0_ffn_W11, L0_ffn_b11, L0_ffn_W2, L0_ffn_b2, L0_ffn_Ws1, L0_ffn_bs1, L0_ffn_Ws11, L0_ffn_bs11, L0_ffn_Ws2, L0_ffn_bs2)
    return x

_drawn_inputs = setup_inputs


def setup_inputs(seed=0):
    import zlib

    import numpy as np

    out = dict(_drawn_inputs(seed))
    spreads = {'L0_xattn_b_Q': (0.0, 0.1),
     'L0_xattn_b_K': (0.0, 2.0),
     'L0_xattn_b_V': (0.0, 0.1),
     'L0_xattn_b_out': (0.0, 0.1)}
    factors = {'L0_ffn_Wg': 8.0,
     'L0_ffn_W1': 8.0,
     'L0_ffn_b1': 8.0,
     'L0_ffn_W11': 8.0,
     'L0_ffn_b11': 8.0,
     'L0_ffn_W2': 8.0,
     'L0_ffn_b2': 34.155,
     'L0_ffn_Ws1': 8.0,
     'L0_ffn_bs1': 8.0,
     'L0_ffn_Ws11': 8.0,
     'L0_ffn_bs11': 8.0,
     'L0_ffn_Ws2': 8.0,
     'L0_ffn_bs2': 25.643}
    for name, (base, spread) in spreads.items():
        noise = np.random.default_rng([zlib.crc32(name.encode()), seed]).standard_normal(out[name].shape)
        drawn = base * np.exp(spread * noise) if base else spread * noise
        out[name] = jnp.asarray(drawn.astype(out[name].dtype))
    for name, factor in factors.items():
        out[name] = (out[name] * factor).astype(out[name].dtype)
    return out
```

```python
from contextlib import ExitStack

import concourse.bass as bass
from concourse import mybir

F32 = mybir.dt.float32
F32R = mybir.dt.float32r
U8 = mybir.dt.uint8
ALU = mybir.AluOpType
ACT = mybir.ActivationFunctionType
AX = mybir.AxisListType

NB, S, D = 16, 100, 128
SK = 1444
H, DK = 16, 64
NE, HID = 16, 256
NX = NE + 2
NTOK = NB * S
EPS = 1e-5
BAND = 64
LOWER, UPPER = BAND // 2, (BAND - 1) // 2
MASKED = -1e30
PAD = -3e38

CB = 4
NC = NB // CB

KT = 12
LASTK = SK - 11 * 128
SHIFT = 128 - LASTK - 4
CW = 362
SKP = 4 * CW
FT = 12
NT = FT + 1
QR = 128 // H
HALF = 64
NG = 6
WIDTH = [256] * 5 + [320]
KPB = [2] * 5 + [1]
STEPS = [(g, k) for g in range(NG) for k in range(0, KT, KPB[g])]
NSTEP = len(STEPS)
PSLOTS = 6
TSLOTS = 3
MSLOTS = 3
PREP = 7


def tiles_of(g):
    return [2 * g, 2 * g + 1] + ([FT] if g == NG - 1 else [])


def rows_of(t):
    return 128 if t < FT else HALF


def group_of(t):
    return min(t // 2, NG - 1)


def steps_to(g):
    return sum(gg <= g for gg, _ in STEPS)


def period():
    split = 27
    steps = [("step", -1, j) for j in range(split, NSTEP)] + [("step", 0, j) for j in range(split)]
    cost = [1.28 if STEPS[j][0] == NG - 1 else 2.05 for _, _, j in steps]
    total, at, out = sum(cost), 0.0, []
    for c, (kind, db, j) in zip(cost, steps):
        out.append(((at + c / 2) / total, kind, db, j))
        at += c
    for n in range(2 * NT):
        out.append(((n + 0.5) / (2 * NT), "score", 0, n))
    out.append((0.41, "project", -1, 0))
    for r, at in enumerate((0.47, 0.54, 0.61, 0.68, 0.75, 0.82, 0.9)):
        out.append((at, "prep", 1, r))
    out.sort()
    return [(n, kind, db, j) for n, (_, kind, db, j) in enumerate(out)]


ORDER = period()
LENGTH = len(ORDER)


def later(items):
    out = []
    for at, kind, db, j in items:
        out.append((at - LENGTH, kind, db - 1, j) if at >= LENGTH else (at, kind, db, j))
    return sorted(out)


def act_order():
    out = []
    for n, kind, db, j in ORDER:
        if kind == "score" and j % 2:
            out.append((n + 1.5, "exp", db, j // 2))
        elif kind == "step":
            out.append((n + 0.1, "step", db, j))
            if STEPS[j][1] + KPB[STEPS[j][0]] == KT:
                out.append((n + 4.2, "out", db, STEPS[j][0]))
        elif kind == "prep":
            out.append((n + 0.3, "prep", db, j))
    return later(out)


def dve_order():
    out = []
    for n, kind, db, j in ORDER:
        if kind == "score":
            out.append((n + 0.2, "score", db, j))
            if j % 2:
                out.append((n + 3.6, "recip", db, j // 2))
        elif kind == "step":
            out.append((n + 1.1, "step", db, j))
            if STEPS[j][1] + KPB[STEPS[j][0]] == KT:
                out.append((n + 5.2, "out", db, STEPS[j][0]))
        elif kind == "prep":
            out.append((n + 0.9, "prep", db, j))
        elif kind == "project":
            out.append((n + 0.9, "project", db, j))
    return later(out)


def pool_order():
    out = []
    for n, kind, db, j in ORDER:
        if kind == "score" and j % 2 == 0:
            t = j // 2 + 1
            out.append((n + 0.5, "bias", db if t < NT else db + 1, t % NT))
        if kind == "score" and j % 2:
            out.append((n + 4.6, "norm", db, j // 2))
        elif kind == "prep" and j >= 3:
            out.append((n + 1.6, "prep", db, j))
    for n in range(3):
        out.append(((0.42 + 0.08 * n) * LENGTH, "split", 1, n))
    return later(out)


def wait_apart(engine, sem, b, per, plus, passed):
    if not isinstance(b, int) or b * per + plus > 0:
        engine.wait_ge(sem, at(b, per, plus))
        if not isinstance(b, int):
            engine.sem_inc(passed, 1)


def at(b, per, plus):
    return b * per + plus


def decoder(nc, x, ctx_in, mask, wq_s, wk_s, wv_s, W_Q, b_Q, W_K, b_K, W_V, b_V, W_out, b_out,
            Wg, W1, b1, W11, b11, W2, b2, Ws1, bs1, Ws11, bs11, Ws2, bs2, out):
    with ExitStack() as whole:
        def psum_banks(n, name):
            return whole.enter_context(nc.psum_tensor(name, [128, n, 512], F32))

        def keep(name, shape, dt=F32):
            return whole.enter_context(nc.sbuf_tensor(name, shape, dt))

        banks = psum_banks(8, "banks")
        ident = keep("ident", [128, 128])
        A_hi, A_lo = keep("A_hi", [128, H, D], F32R), keep("A_lo", [128, H, D], F32R)
        VO_hi, VO_lo = keep("VO_hi", [128, H, D], F32R), keep("VO_lo", [128, H, D], F32R)
        u = keep("u", [128, H])
        c_all = keep("c_all", [128, NB, NT])
        x1_dram = nc.dram_tensor("x1_dram", (NB, S, D), F32, kind="Internal").ap()
        n2hi_dram = nc.dram_tensor("n2hi_dram", (NB, D, S), F32, kind="Internal").ap()
        n2lo_dram = nc.dram_tensor("n2lo_dram", (NB, D, S), F32, kind="Internal").ap()
        x2_dram = nc.dram_tensor("x2_dram", (NTOK, D), F32, kind="Internal").ap()

        self_attention(nc, x, wq_s, wk_s, wv_s, W_Q, b_Q, W_K, b_K, W_V, b_V, W_out, b_out,
                       banks, ident, A_hi, A_lo, VO_hi, VO_lo, u, c_all,
                       x1_dram, n2hi_dram, n2lo_dram)
        cross_attention(nc, ctx_in, mask, banks, ident, A_hi, A_lo, VO_hi, VO_lo, u, c_all,
                        x1_dram, n2hi_dram, n2lo_dram, x2_dram)
        experts(nc, Wg, W1, b1, W11, b11, W2, b2, Ws1, bs1, Ws11, bs11, Ws2, bs2,
                banks, ident, x2_dram, out)


class Chain:

    def __init__(self, engine, sem):
        self.engine, self.sem, self.count = engine, sem, 0

    def __call__(self, ins):
        ins.then_inc(self.sem, 1)
        self.count += 1
        self.engine.wait_ge(self.sem, self.count)


def self_attention(nc, x, wq_s, wk_s, wv_s, W_Q, b_Q, W_K, b_K, W_V, b_V, W_out, b_out,
                   banks, ident, A_hi, A_lo, VO_hi, VO_lo, u, c_all,
                   x1_dram, n2hi_dram, n2lo_dram):
    with ExitStack() as ctx:
        def sb(name, shape, dt=F32):
            return ctx.enter_context(nc.sbuf_tensor(name, shape, dt))

        def sem(name):
            return ctx.enter_context(nc.semaphore(name))

        xt = sb("xt", [S, NB, D])
        cen, nrm = sb("cen", [S, NB, D]), sb("nrm", [S, NB, D])
        sq = sb("sq", [S, CB, D])
        st = sb("st", [S, 8, NB])
        xnT = sb("xnT", [128, NTOK])
        qT, kT = sb("qT", [128, NTOK]), sb("kT", [128, NTOK])
        v = sb("v", [S, NB, D])
        pr = sb("pr", [S, NB, S])
        prT = sb("prT", [S, NB, S])
        band = sb("band", [S, S])
        n2hi, n2lo = sb("n2hi", [128, NTOK], F32R), sb("n2lo", [128, NTOK], F32R)
        wsq, wsk, wsv = sb("wsq", [D, D]), sb("wsk", [D, D]), sb("wsv", [D, D])
        wQ, wK, wV = sb("wQ", [DK, H, D]), sb("wK", [DK, H, D]), sb("wV", [DK, H, D])
        wo = sb("wo", [D, H * DK])
        woT = sb("woT", [DK, H, D])
        bQ, bK, bV = sb("bQ", [DK, H]), sb("bK", [DK, H]), sb("bV", [DK, H])
        bo = sb("bo", [1, D])
        bVrep = sb("bVrep", [DK, H, S])
        bb = sb("bb", [DK, H])
        bbrep = sb("bbrep", [DK, QR, H])
        ones = sb("ones", [DK, S])
        wpad = sb("wpad", [128, 2 * 128 - H])
        kcol = sb("kcol", [128, 1])
        const_row = sb("const_row", [S, D])
        rmax, rsum, rinv = sb("rmax", [S, NB]), sb("rsum", [S, NB]), sb("rinv", [S, NB])

        x_in, wqk_in, wv_in = sem("x_in"), sem("wqk_in"), sem("wv_in")
        self_in = sem("self_in")
        consts = sem("consts")
        dve_chain, pool_chain = sem("dve_chain"), sem("pool_chain")
        squared, var_ready, std_ready = sem("squared"), sem("var_ready"), sem("std_ready")
        centered = sem("centered")
        normed = sem("normed")
        xT_ready, xT_copied = sem("xT_ready"), sem("xT_copied")
        q_ready, k_ready, v_ready = sem("q_ready"), sem("k_ready"), sem("v_ready")
        q_copied, k_copied, v_copied = sem("q_copied"), sem("k_copied"), sem("v_copied")
        s_ready, s_shifted, s_exp = sem("s_ready"), sem("s_shifted"), sem("s_exp")
        pT_ready, pT_copied = sem("pT_ready"), sem("pT_copied")
        o_ready, x1_ready = sem("o_ready"), sem("x1_ready")
        nT_ready, nT_hi, nT_lo = sem("nT_ready"), sem("nT_hi"), sem("nT_lo")
        w_ready, w_hi, w_done = sem("w_ready"), sem("w_hi"), sem("w_done")
        bias_made = sem("bias_made")
        stored = sem("stored")

        def cols(c):
            return slice(c * CB * S, (c + 1) * CB * S)

        def chunk(t, c):
            return t[:, c * CB:(c + 1) * CB, :]

        def bank(n, rows=128, width=512, a=None):
            p = banks[0:rows, n, 0:width]
            return p if a is None else p.rearrange("p (a n) -> p a n", a=a)

        def wbank(r):
            return 4 + r % 4

        R_SMALL, R_WOT, R_A, R_VO, R_CONST, R_C = 0, 1, 5, 9, 13, 14

        with nc.Block() as block:
            @block.sync
            def _(sp):
                for c in range(NC):
                    sp.dma_start(chunk(xt, c), x[c * CB:(c + 1) * CB].rearrange("b q d -> q b d"))\
                        .then_inc(x_in, 16)
                for t, w in ((wsq, wq_s), (wsk, wk_s), (wsv, wv_s)):
                    sp.dma_start(t[:, :], w).then_inc(self_in, 16)
                for c in range(NC):
                    sp.wait_ge(x1_ready, c + 1)
                    sp.dma_start(x1_dram[c * CB:(c + 1) * CB].rearrange("b q d -> q b d"), chunk(xt, c))\
                        .then_inc(stored, 16)
                    sp.wait_ge(nT_lo, c + 1)
                    for t, w in ((n2hi, n2hi_dram), (n2lo, n2lo_dram)):
                        sp.dma_start(w[c * CB:(c + 1) * CB].rearrange("b d q -> d b q"),
                                     t[:, cols(c)].bitcast(F32).rearrange("p (b q) -> p b q", b=CB))\
                            .then_inc(stored, 16)
                sp.wait_ge(stored, 16 * 3 * NC)

            @block.gpsimd
            def _(pool):
                link = Chain(pool, pool_chain)
                link(pool.memset(ident[:, :], 0.0))
                pool.affine_select(out=ident[:, :], in_=ident[:, :], compare_op=ALU.not_equal, fill=1.0,
                                   base=0, pattern=[[-1, 128]], channel_multiplier=1).then_inc(consts, 1)
                link(pool.memset(band[:, :], float(D) ** -0.5))
                link(pool.affine_select(out=band[:, :], in_=band[:, :], compare_op=ALU.is_ge, fill=0.0,
                                        base=LOWER, pattern=[[1, S]], channel_multiplier=-1))
                pool.affine_select(out=band[:, :], in_=band[:, :], compare_op=ALU.is_ge, fill=0.0,
                                   base=UPPER, pattern=[[-1, S]], channel_multiplier=1).then_inc(consts, 1)
                pool.memset(ones[:, :], 1.0).then_inc(consts, 1)
                pool.memset(wpad[:, :], 0.0).then_inc(consts, 1)
                pool.wait_ge(wqk_in, 16 * 4)
                link(pool.tensor_tensor(bb[:, :], bQ[:, :], bK[:, :], ALU.mult))
                pool.tensor_copy(bbrep[:, :, :], bb[:, :].unsqueeze(1).to_broadcast([DK, QR, H]))\
                    .then_inc(bias_made, 1)
                pool.wait_ge(wv_in, 16 * 4)
                pool.tensor_copy(bVrep[:, :, :], bV[:, :].unsqueeze(2).to_broadcast([DK, H, S]))\
                    .then_inc(bias_made, 1)

            @block.scalar
            def _(act):
                for t, w in ((wQ, W_Q), (wK, W_K)):
                    act.dma_start(t[:, :, :], w.rearrange("(h j) d -> j h d", j=DK)).then_inc(wqk_in, 16)
                for t, w in ((bQ, b_Q), (bK, b_K)):
                    act.dma_start(t[:, :], w.rearrange("(h j) -> j h", j=DK), allow_slow_non_contiguous=True).then_inc(wqk_in, 16)
                act.dma_start(wo[:, :], W_out).then_inc(wv_in, 16)
                act.dma_start(wV[:, :, :], W_V.rearrange("(h j) d -> j h d", j=DK)).then_inc(wv_in, 16)
                act.dma_start(bV[:, :], b_V.rearrange("(h j) -> j h", j=DK), allow_slow_non_contiguous=True).then_inc(wv_in, 16)
                act.dma_start(bo[:, :], b_out.rearrange("(a d) -> a d", a=1)).then_inc(wv_in, 16)

                def std(n):
                    act.wait_ge(var_ready, n + 1)
                    act.activation(st[:, 3, (n % NC) * CB:(n % NC + 1) * CB],
                                   st[:, 2, (n % NC) * CB:(n % NC + 1) * CB], ACT.Sqrt).then_inc(std_ready, 1)

                for c in range(NC):
                    std(c)
                for c in range(NC):
                    act.wait_ge(xT_ready, c + 1)
                    act.copy(xnT[:, cols(c)], bank(c, width=CB * S)).then_inc(xT_copied, 1)

                def split_hi(n, r, dst, src_a=4):
                    act.wait_ge(w_ready, r + 1)
                    scale = 0.125 if dst is A_hi else 1.0
                    act.activation(dst[:, 4 * n:4 * n + 4, :], bank(wbank(r), a=4), ACT.Copy, scale=scale)\
                        .then_inc(w_hi, 1)

                for n in range(4):
                    split_hi(n, R_A + n, A_hi)
                for n in range(4):
                    split_hi(n, R_VO + n, VO_hi)
                for c in range(NC):
                    act.wait_ge(q_ready, c + 1)
                    act.copy(qT[:, cols(c)], bank(c, width=CB * S)).then_inc(q_copied, 1)
                for c in range(NC):
                    act.wait_ge(v_ready, c + 1)
                    act.copy(chunk(v, c), bank(c, S, a=CB)).then_inc(v_copied, 1)
                for c in range(NC):
                    act.wait_ge(s_shifted, c + 1)
                    act.activation(chunk(pr, c), chunk(pr, c), ACT.Exp).then_inc(s_exp, 1)
                for c in range(NC):
                    act.wait_ge(pT_ready, c + 1)
                    act.copy(chunk(prT, c), bank(c, S, CB * S, a=CB)).then_inc(pT_copied, 1)
                for c in range(NC):
                    std(NC + c)
                for c in range(NC):
                    act.wait_ge(nT_ready, c + 1)
                    act.copy(n2hi[:, cols(c)], bank(c, width=CB * S)).then_inc(nT_hi, 1)

            @block.vector
            def _(dve):
                link = Chain(dve, dve_chain)

                def norm(c, n):
                    cs = slice(c * CB, (c + 1) * CB)
                    wide = [S, CB, D]
                    link(dve.tensor_reduce(st[:, 0, cs], chunk(xt, c), AX.X, ALU.add))
                    link(dve.tensor_scalar(st[:, 1, cs], st[:, 0, cs], 1.0 / D, None, ALU.mult))
                    link(dve.tensor_tensor(chunk(cen, c), chunk(xt, c),
                                           st[:, 1, cs].unsqueeze(2).to_broadcast(wide), ALU.subtract))
                    link(dve.tensor_tensor(sq[:, :, :], chunk(cen, c), chunk(cen, c), ALU.mult))
                    link(dve.tensor_reduce(st[:, 0, cs], sq[:, :, :], AX.X, ALU.add))
                    dve.tensor_scalar(st[:, 2, cs], st[:, 0, cs], 1.0 / D, EPS, ALU.mult, ALU.add)\
                        .then_inc(var_ready, 1)

                def scale(c, n):
                    cs = slice(c * CB, (c + 1) * CB)
                    dve.wait_ge(std_ready, n + 1)
                    link(dve.reciprocal(st[:, 4, cs], st[:, 3, cs]))
                    dve.tensor_tensor(chunk(nrm, c), chunk(cen, c),
                                      st[:, 4, cs].unsqueeze(2).to_broadcast([S, CB, D]), ALU.mult)\
                        .then_inc(normed, 1)

                for c in range(NC):
                    dve.wait_ge(x_in, 16 * NC)
                    norm(c, c)
                for c in range(NC):
                    scale(c, c)

                dve.wait_ge(w_ready, R_SMALL + 1)
                dve.wait_ge(consts, 4)
                dve.tensor_scalar(u[:, :], bank(wbank(R_SMALL))[:, 0:H], 0.125, None, ALU.mult)
                dve.tensor_copy(wpad[:, 128 - H:128], bank(wbank(R_SMALL))[:, H:2 * H])
                dve.tensor_copy(kcol[:, :], bank(wbank(R_SMALL))[:, 2 * H:2 * H + 1]).then_inc(w_done, 1)
                for n in range(4):
                    dve.wait_ge(w_ready, R_WOT + n + 1)
                    dve.tensor_copy(woT[:, 4 * n:4 * n + 4, :], bank(wbank(R_WOT + n), DK, a=4)).then_inc(w_done, 1)
                for n in range(4):
                    dve.wait_ge(w_hi, n + 1)
                    dve.scalar_tensor_tensor(A_lo[:, 4 * n:4 * n + 4, :], bank(wbank(R_A + n), a=4), 0.125,
                                             A_hi[:, 4 * n:4 * n + 4, :].bitcast(F32), ALU.mult, ALU.subtract)\
                        .then_inc(w_done, 1)
                for n in range(4):
                    dve.wait_ge(w_hi, 4 + n + 1)
                    dve.tensor_tensor(VO_lo[:, 4 * n:4 * n + 4, :], bank(wbank(R_VO + n), a=4),
                                      VO_hi[:, 4 * n:4 * n + 4, :].bitcast(F32), ALU.subtract).then_inc(w_done, 1)
                dve.wait_ge(w_ready, R_CONST + 1)
                dve.tensor_copy(const_row[:, :], bank(wbank(R_CONST), S, D)).then_inc(w_done, 1)

                for c in range(NC):
                    dve.wait_ge(k_ready, c + 1)
                    dve.tensor_copy(kT[:, cols(c)], bank(4 + c, width=CB * S)).then_inc(k_copied, 1)
                for c in range(NC):
                    cs = slice(c * CB, (c + 1) * CB)
                    dve.wait_ge(s_ready, c + 1)
                    link(dve.tensor_tensor(chunk(pr, c), bank(4 + c, S, CB * S, a=CB),
                                           band[:, :].unsqueeze(1).to_broadcast([S, CB, S]), ALU.mult))
                    link(dve.tensor_reduce(rmax[:, cs], chunk(pr, c), AX.X, ALU.max))
                    dve.tensor_tensor(chunk(pr, c), chunk(pr, c),
                                      rmax[:, cs].unsqueeze(2).to_broadcast([S, CB, S]), ALU.subtract)\
                        .then_inc(s_shifted, 1)
                for c in range(NC):
                    cs = slice(c * CB, (c + 1) * CB)
                    dve.wait_ge(s_exp, c + 1)
                    link(dve.tensor_reduce(rsum[:, cs], chunk(pr, c), AX.X, ALU.add))
                    link(dve.reciprocal(rinv[:, cs], rsum[:, cs]))
                for c in range(NC):
                    dve.wait_ge(o_ready, c + 1)
                    for n in range(CB):
                        b = c * CB + n
                        last = dve.scalar_tensor_tensor(xt[:, b, :], bank(4 + c, S, a=CB)[:, n, :], rinv[:, b:b + 1],
                                                        xt[:, b, :], ALU.mult, ALU.add)
                    link(last)
                    norm(c, NC + c)
                for c in range(NC):
                    scale(c, NC + c)
                for c in range(NC):
                    dve.tensor_tensor(chunk(xt, c), chunk(xt, c),
                                      const_row[:, :].unsqueeze(1).to_broadcast([S, CB, D]), ALU.add)\
                        .then_inc(x1_ready, 1)
                for c in range(NC):
                    dve.wait_ge(nT_hi, c + 1)
                    dve.tensor_tensor(n2lo[:, cols(c)], bank(c, width=CB * S), n2hi[:, cols(c)].bitcast(F32),
                                      ALU.subtract).then_inc(nT_lo, 1)
                dve.wait_ge(w_ready, R_C + 1)
                dve.tensor_scalar(c_all[:, :, 0:FT], bank(4, width=NB * FT, a=NB), kcol[:, 0:1], 0.125,
                                  ALU.add, ALU.mult)
                link(dve.tensor_scalar(c_all[:, :, FT:NT], bank(5, width=NB, a=NB), kcol[:, 0:1], 0.125,
                                       ALU.add, ALU.mult))

            @block.tensor
            def _(pe):
                pe.wait_ge(consts, 1)
                for c in range(NC):
                    pe.wait_ge(normed, c + 1)
                    for n in range(CB):
                        last = pe.transpose(bank(c)[:, n * S:(n + 1) * S], nrm[:, c * CB + n, :], ident[0:S, 0:S])
                    last.then_inc(xT_ready, 1)

                def w_free(r):
                    if r >= 4:
                        pe.wait_ge(w_done, r - 3)

                pe.wait_ge(wqk_in, 16 * 4)
                pe.wait_ge(bias_made, 1)
                pe.wait_ge(consts, 4)
                small = bank(wbank(R_SMALL))
                for h in range(H):
                    pe.matmul(small[:, h:h + 1], wK[:, h, :], bQ[:, h:h + 1], start=True, stop=True)
                    pe.matmul(small[:, H + h:H + h + 1], wQ[:, h, :], bK[:, h:h + 1], start=True, stop=True)
                pe.matmul(small[:, 2 * H:2 * H + 1], bbrep[:, :, :].rearrange("j q h -> j (q h)"), ones[:, 0:1],
                          start=True, stop=True).then_inc(w_ready, 1)
                pe.wait_ge(wv_in, 16 * 4)
                for n in range(4):
                    w_free(R_WOT + n)
                    for i in range(4):
                        h = 4 * n + i
                        last = pe.transpose(bank(wbank(R_WOT + n), DK, a=4)[:, i, :], wo[:, h * DK:(h + 1) * DK],
                                            ident[:, :])
                    last.then_inc(w_ready, 1)
                for n in range(4):
                    w_free(R_A + n)
                    for i in range(4):
                        h = 4 * n + i
                        last = pe.matmul(bank(wbank(R_A + n), a=4)[:, i, :], wQ[:, h, :], wK[:, h, :],
                                         start=True, stop=True)
                    last.then_inc(w_ready, 1)
                pe.wait_ge(w_done, R_WOT + 4)
                for n in range(4):
                    w_free(R_VO + n)
                    for i in range(4):
                        h = 4 * n + i
                        last = pe.matmul(bank(wbank(R_VO + n), a=4)[:, i, :], wV[:, h, :], woT[:, h, :],
                                         start=True, stop=True)
                    last.then_inc(w_ready, 1)
                w_free(R_CONST)
                pe.wait_ge(bias_made, 2)
                for h in range(H):
                    pe.matmul(bank(wbank(R_CONST), S, D), bVrep[:, h, :], woT[:, h, :], start=(h == 0), stop=False)
                pe.matmul(bank(wbank(R_CONST), S, D), ones[0:1, :], bo[:, :], start=False, stop=True)\
                    .then_inc(w_ready, 1)

                pe.wait_ge(self_in, 16 * 3)
                for c in range(NC):
                    pe.wait_ge(xT_copied, c + 1)
                    pe.matmul(bank(c, width=CB * S), wsq[:, :], xnT[:, cols(c)], start=True, stop=True)\
                        .then_inc(q_ready, 1)
                pe.wait_ge(w_done, R_CONST + 1)
                for c in range(NC):
                    pe.matmul(bank(4 + c, width=CB * S), wsk[:, :], xnT[:, cols(c)], start=True, stop=True)\
                        .then_inc(k_ready, 1)
                for c in range(NC):
                    pe.wait_ge(q_copied, c + 1)
                    for n in range(CB):
                        b = c * CB + n
                        last = pe.matmul(bank(c, S, a=CB)[:, n, :], xnT[:, b * S:(b + 1) * S], wsv[:, :],
                                         start=True, stop=True)
                    last.then_inc(v_ready, 1)
                for c in range(NC):
                    pe.wait_ge(k_copied, c + 1)
                    for n in range(CB):
                        b = c * CB + n
                        last = pe.matmul(bank(4 + c, S, CB * S, a=CB)[:, n, :], qT[:, b * S:(b + 1) * S],
                                         kT[:, b * S:(b + 1) * S], start=True, stop=True)
                    last.then_inc(s_ready, 1)
                for c in range(NC):
                    pe.wait_ge(v_copied, c + 1)
                    pe.wait_ge(s_exp, c + 1)
                    for n in range(CB):
                        last = pe.transpose(bank(c, S, CB * S, a=CB)[:, n, :], pr[:, c * CB + n, :],
                                            ident[0:S, 0:S])
                    last.then_inc(pT_ready, 1)
                for c in range(NC):
                    pe.wait_ge(pT_copied, c + 1)
                    pe.wait_ge(s_shifted, c + 1)
                    for n in range(CB):
                        b = c * CB + n
                        last = pe.matmul(bank(4 + c, S, a=CB)[:, n, :], prT[:, b, :], v[:, b, :],
                                         start=True, stop=True)
                    last.then_inc(o_ready, 1)
                for c in range(NC):
                    pe.wait_ge(normed, NC + c + 1)
                    for n in range(CB):
                        last = pe.transpose(bank(c)[:, n * S:(n + 1) * S], nrm[:, c * CB + n, :], ident[0:S, 0:S])
                    last.then_inc(nT_ready, 1)
                pe.wait_ge(nT_lo, NC)
                pe.wait_ge(w_done, 1)

                def c_rows(dst, first, n, step, offsets):
                    for part, xs in enumerate((n2hi, n2lo)):
                        xv = xs[:, :].bitcast(F32).rearrange("p (b q) -> p b q", b=NB)
                        for j in offsets:
                            xj = xv[:, :, first + j:first + j + step * (n - 1) + 1:step]
                            last = pe.matmul(dst, wpad[:, 128 - H - H * j:256 - H - H * j], xj,
                                             start=(part == 0 and j == 0), stop=(part == 1 and j == offsets[-1]))
                    return last

                c_rows(bank(4, width=NB * FT, a=NB), 0, FT, QR, range(QR))
                c_rows(bank(5, width=NB, a=NB), FT * QR, 1, 1, range(S - FT * QR)).then_inc(w_ready, 1)


def cross_attention(nc, ctx_in, mask, banks, ident, A_hi, A_lo, VO_hi, VO_lo, u, c_all,
                    x1_dram, n2hi_dram, n2lo_dram, x2_dram):
    with ExitStack() as ctx:
        def sb(name, shape, dt=F32):
            return ctx.enter_context(nc.sbuf_tensor(name, shape, dt))

        def sem(name):
            return ctx.enter_context(nc.semaphore(name))

        def pair(name, shape, dt=F32):
            return [sb(f"{name}{i}", shape, dt) for i in range(2)]

        nat = sb("nat", [128, KT, D])
        ctx_hi, ctx_lo = pair("ctx_hi", [128, KT, D], F32R), pair("ctx_lo", [128, KT, D], F32R)
        ctxT_hi, ctxT_lo = pair("ctxT_hi", [128, SKP], F32R), pair("ctxT_lo", [128, SKP], F32R)
        qh, ql = pair("qh", [128, NT * 128], F32R), pair("ql", [128, NT * 128], F32R)
        qf = sb("qf", [128, 4, S])
        n2h, n2l = pair("n2h", [128, S], F32R), pair("n2l", [128, S], F32R)
        x1, x2 = pair("x1", [S, D]), pair("x2", [S, D])
        masks = [sb(f"mask{i}", [128, SK], U8) for i in range(MSLOTS)]
        mask_half = sb("mask_half", [HALF, SK], U8)
        bias = pair("bias", [128, SKP])
        probs = [sb(f"probs{i}", [128, SKP]) for i in range(PSLOTS)]
        probs_half = sb("probs_half", [HALF, SKP])
        pT_hi = [sb(f"pT_hi{i}", [128, 512], F32R) for i in range(TSLOTS)]
        pT_lo = [sb(f"pT_lo{i}", [128, 512], F32R) for i in range(TSLOTS)]
        oT_hi, oT_lo = sb("oT_hi", [128, S * H], F32R), sb("oT_lo", [128, S * H], F32R)
        c_cur = pair("c_cur", [128, NT])
        nmax = sb("nmax", [128, 2, PSLOTS + 1])
        rsum = sb("row_sum", [128, PSLOTS + 1])
        rinv = sb("row_inv", [128, PSLOTS + 1])

        zeroed = sem("zeroed")
        nat_in = sem("nat_in")
        passed_sp, passed_pool, passed_dve = sem("passed_sp"), sem("passed_pool"), sem("passed_dve")
        rows_in = [sem("rows_in0"), sem("rows_in1")]
        x1_in = [sem("x1_in0"), sem("x1_in1")]
        mask_in = [sem(f"mask_in{i}") for i in range(MSLOTS)]
        mask_half_in = sem("mask_half_in")
        c_here = sem("c_here")
        ctx_split = sem("ctx_split")
        ctx_hi_made = sem("ctx_hi_made")
        bias_ready = sem("bias_ready")
        scores_ready, scores_taken = sem("scores_ready"), sem("scores_taken")
        exp_done, recip_done, probs_ready = sem("exp_done"), sem("recip_done"), sem("probs_ready")
        turned, turned_hi, turned_lo = sem("turned"), sem("turned_hi"), sem("turned_lo")
        values_done = sem("values_done")
        out_hi, out_lo = sem("out_hi"), sem("out_lo")
        prep_ready, prep_hi, prep_read = sem("prep_ready"), sem("prep_hi"), sem("prep_read")
        q_split = sem("q_split")
        qf_used = sem("qf_used")
        proj_ready, x2_ready, x2_stored = sem("proj_ready"), sem("x2_ready"), sem("x2_stored")

        S_BANK, T_BANK, O_BANK, MISC = 0, 4, 6, 7

        def slot(t):
            return t % PSLOTS if t < FT else PSLOTS

        def prob(t):
            return probs[t % PSLOTS] if t < FT else probs_half

        def known(b):
            return isinstance(b, int)

        def here(b, db):
            return not known(b) or 0 <= b + db < NB

        def wait(engine, sem, b, per, plus):
            if not known(b) or b * per + plus > 0:
                engine.wait_ge(sem, at(b, per, plus))

        def periods(engine, emit):
            emit(-1, 1)
            emit(0, 0)
            with engine.Fori(1, NB - 2, 2) as b:
                emit(b, 1)
                emit(b + 1, 0)
            emit(NB - 1, 1)
            emit(NB, 0)

        with nc.Block() as block:
            @block.sync
            def _(sp):
                sp.wait_ge(zeroed, 2 * 3 + 1)

                def load_rows(b, odd):
                    wait_apart(sp, ctx_split, b, 3, 0, passed_sp)
                    wait_apart(sp, prep_ready, b, PREP, 3 - PREP, passed_sp)
                    c = ctx_in[b] if known(b) else ctx_in[bass.ds(b, 1)].rearrange("a k d -> (a k) d")
                    sp.dma_start(nat[:, 0:KT - 1, :], c[0:(KT - 1) * 128, :].rearrange("(t p) d -> p t d", p=128))\
                        .then_inc(nat_in, 16)
                    sp.dma_start(nat[SHIFT:SHIFT + LASTK, KT - 1, :], c[(KT - 1) * 128:SK, :]).then_inc(nat_in, 16)
                    for t, w in ((n2h, n2hi_dram), (n2l, n2lo_dram)):
                        wait_apart(sp, prep_ready, b, PREP, -PREP, passed_sp)
                        w_b = w[b] if known(b) else w[bass.ds(b, 1)].rearrange("a k d -> (a k) d")
                        sp.dma_start(t[odd][:, :].bitcast(F32), w_b).then_inc(rows_in[odd], 16)

                def load_x1(b, odd):
                    x_b = x1_dram[b] if known(b) else x1_dram[bass.ds(b, 1)].rearrange("a k d -> (a k) d")
                    sp.dma_start(x1[odd][:, :], x_b).then_inc(x1_in[odd], 16)

                def load_mask(b, t):
                    q0, nq = t * QR, rows_of(t) // H
                    if known(b):
                        src = mask[b, q0:q0 + nq, :]
                    else:
                        src = mask[bass.ds(b, 1), q0:q0 + nq, :].rearrange("a q k -> (a q) k")
                    dst = masks[t % MSLOTS] if t < FT else mask_half
                    if t < FT:
                        before = t - MSLOTS + 1 if t >= MSLOTS else t - MSLOTS - 1 + 1
                        wait_apart(sp, bias_ready, b, NT, before, passed_sp)
                    else:
                        wait_apart(sp, bias_ready, b, NT, 0, passed_sp)
                    sp.dma_start(dst[:, :], src.unsqueeze(1).to_broadcast([nq, H, SK]))\
                        .then_inc(mask_in[t % MSLOTS] if t < FT else mask_half_in, 16)

                def emit(b, odd):
                    if here(b, 1):
                        load_rows(b + 1, 1 - odd)
                    if known(b) and b < 0:
                        load_x1(0, 0)
                    for t in range(NT):
                        if here(b, 0):
                            load_mask(b, t)
                        if t == 9 and here(b, -1):
                            wait_apart(sp, x2_ready, b, 1, 0, passed_sp)
                            dst = x2_dram[bass.ds((b - 1) * S, S), :] if not known(b) else \
                                x2_dram[(b - 1) * S:b * S, :]
                            sp.dma_start(dst, x2[1 - odd][:, :]).then_inc(x2_stored, 16)
                    if here(b, 0) and here(b, 1):
                        wait_apart(sp, x2_stored, b, 16, 0, passed_sp)
                        load_x1(b + 1, 1 - odd)

                periods(sp, emit)
                sp.wait_ge(x2_stored, 16 * NB)

            @block.gpsimd
            def _(pool):
                pool.memset(nat[:, KT - 1, :], 0.0).then_inc(zeroed, 1)
                for i in range(2):
                    pool.memset(bias[i][:, SK:SKP], PAD).then_inc(zeroed, 1)
                    for t in (qh, ql):
                        pool.memset(t[i][:, S * H:NT * 128].bitcast(F32), 0.0).then_inc(zeroed, 1)

                order = pool_order()

                def emit(b, odd):
                    def make_bias(db, t):
                        i = odd if db == 0 else 1 - odd
                        n = rows_of(t)
                        if t == 0:
                            b_abs = b + db
                            wait(pool, bias_ready, b_abs, NT, -NT)
                            src = c_all[:, b_abs, :] if known(b_abs) else \
                                c_all[:, bass.ds(b_abs, 1), :].rearrange("p a t -> p (a t)")
                            pool.tensor_copy(c_cur[i][:, :], src).then_inc(c_here, 1)
                            wait(pool, c_here, b_abs, 1, 1)
                        if t < FT:
                            wait(pool, mask_in[t % MSLOTS], b + db, 16 * (FT // MSLOTS), 16 * (t // MSLOTS + 1))
                        else:
                            wait(pool, mask_half_in, b + db, 16, 16)
                        wait_apart(pool, scores_taken, b + db, 2 * NT, 2 * (t - 1), passed_pool)
                        src = masks[t % MSLOTS] if t < FT else mask_half
                        pool.tensor_scalar(bias[(t + i) % 2][0:n, 0:SK], src[:, :], MASKED, c_cur[i][0:n, t:t + 1],
                                           ALU.mult, ALU.add).then_inc(bias_ready, 1)

                    for _, kind, db, j in order:
                        if not here(b, db):
                            continue
                        if kind == "bias":
                            make_bias(db, j)
                        elif kind == "norm":
                            wait_apart(pool, recip_done, b + db, NT, j + 1, passed_pool)
                            n, s = rows_of(j), slot(j)
                            pool.tensor_scalar(prob(j)[0:n, :], prob(j)[0:n, :], rinv[0:n, s:s + 1], 1.0,
                                               ALU.mult, ALU.mult).then_inc(probs_ready, 1)
                        elif kind == "split":
                            i = 1 - odd
                            part = slice(4 * j, 4 * j + 4)
                            if j == 0:
                                wait(pool, values_done, b + db, NSTEP, -NSTEP)
                                wait_apart(pool, nat_in, b + db, 32, 32, passed_pool)
                            pool.tensor_scalar(ctx_hi[i][:, part, :], nat[:, part, :], 1.0, 1.0, ALU.mult, ALU.mult)\
                                .then_inc(ctx_hi_made, 1)
                            wait(pool, ctx_hi_made, b + db, 3, j + 1)
                            pool.tensor_tensor(ctx_lo[i][:, part, :], nat[:, part, :],
                                               ctx_hi[i][:, part, :].bitcast(F32), ALU.subtract)\
                                .then_inc(ctx_split, 1)
                        elif kind == "prep":
                            i, n = 1 - odd, j - 3
                            wait(pool, prep_hi, b + db, PREP, j + 1)
                            dst = ql[i][:, 0:S * H].rearrange("p (q h) -> p h q", h=H)[:, 4 * n:4 * n + 4, :]
                            hi = qh[i][:, 0:S * H].rearrange("p (q h) -> p h q", h=H)[:, 4 * n:4 * n + 4, :]
                            pool.tensor_tensor(dst, qf[:, :, :], hi.bitcast(F32), ALU.subtract)\
                                .then_inc(q_split, 1)

                def start():
                    pool.wait_ge(zeroed, 2 * 3 + 1)

                start()
                periods(pool, emit)

            @block.scalar
            def _(act):
                order = act_order()

                def emit(b, odd):
                    for _, kind, db, j in order:
                        if not here(b, db):
                            continue
                        i = odd if db == 0 else 1 - odd
                        if kind == "exp":
                            n, s = rows_of(j), slot(j)
                            wait(act, scores_taken, b + db, 2 * NT, 2 * j + 2)
                            act.activation(prob(j)[0:n, :], prob(j)[0:n, :], ACT.Exp,
                                           bias=nmax[0:n, 1, s:s + 1], scale=-1.0,
                                           accum_out=rsum[0:n, s:s + 1]).then_inc(exp_done, 1)
                        elif kind == "step":
                            g, _ = STEPS[j]
                            w = WIDTH[g] * KPB[g]
                            wait(act, turned, b + db, NSTEP, j + 1)
                            wait(act, values_done, b + db, NSTEP, j + 1 - TSLOTS)
                            act.copy(pT_hi[j % TSLOTS][:, 0:w], banks[:, T_BANK + j % 2, 0:w]).then_inc(turned_hi, 1)
                        elif kind == "out":
                            wait(act, values_done, b + db, NSTEP, steps_to(j))
                            wait(act, proj_ready, b + db, 1, 0)
                            cs = slice(256 * j, 256 * j + WIDTH[j])
                            act.copy(oT_hi[:, cs], banks[:, O_BANK, 0:WIDTH[j]]).then_inc(out_hi, 1)
                        elif kind == "prep":
                            if j < 3:
                                wait(act, prep_ready, b + db, PREP, j + 1)
                                w = min(512, SKP - 512 * j)
                                src = banks[:, MISC, 0:512]
                                if j == 2:
                                    act.copy(ctxT_hi[i][:, 1024:1408], src[:, 0:384])
                                    act.copy(ctxT_hi[i][:, 1408:SKP], src[:, 384 + SHIFT:512]).then_inc(prep_hi, 1)
                                else:
                                    act.copy(ctxT_hi[i][:, 512 * j:512 * j + w], src[:, 0:w]).then_inc(prep_hi, 1)
                            else:
                                wait(act, prep_read, b + db, PREP, j + 1)
                                n = j - 3
                                dst = qh[i][:, 0:S * H].rearrange("p (q h) -> p h q", h=H)[:, 4 * n:4 * n + 4, :]
                                act.copy(dst, qf[:, :, :]).then_inc(prep_hi, 1)

                periods(act, emit)

            @block.vector
            def _(dve):
                order = dve_order()

                def emit(b, odd):
                    for _, kind, db, j in order:
                        if not here(b, db):
                            continue
                        i = odd if db == 0 else 1 - odd
                        if kind == "score":
                            t, half = j // 2, j % 2
                            n, s = rows_of(t), slot(t)
                            if half == 0:
                                wait(dve, bias_ready, b + db, NT, t + 1)
                                if t >= FT:
                                    wait(dve, turned, b + db, NSTEP, 0)
                                elif t >= PSLOTS:
                                    wait(dve, turned, b + db, NSTEP, steps_to(group_of(t - PSLOTS)))
                                else:
                                    wait(dve, turned, b + db, NSTEP, steps_to(group_of(t + PSLOTS)) - NSTEP)
                            else:
                                wait(dve, scores_taken, b + db, 2 * NT, j)
                            wait_apart(dve, scores_ready, b + db, 2 * NT, j + 1, passed_dve)
                            cs = slice(half * 2 * CW, (half + 1) * 2 * CW)
                            src = banks[0:n, S_BANK + 2 * half:S_BANK + 2 * half + 2, 0:CW]
                            first = -PAD if half == 0 else nmax[0:n, 0, s:s + 1]
                            dve.tensor_tensor_reduce(
                                prob(t)[0:n, cs].rearrange("p (a k) -> p a k", a=2), src,
                                bias[(t + i) % 2][0:n, cs].rearrange("p (a k) -> p a k", a=2), -1.0, first,
                                ALU.add, ALU.min, nmax[0:n, half, s:s + 1]).then_inc(scores_taken, 1)
                        elif kind == "recip":
                            n, s = rows_of(j), slot(j)
                            wait(dve, exp_done, b + db, NT, j + 1)
                            dve.reciprocal(rinv[0:n, s:s + 1], rsum[0:n, s:s + 1]).then_inc(recip_done, 1)
                        elif kind == "step":
                            g, _ = STEPS[j]
                            w = WIDTH[g] * KPB[g]
                            wait(dve, turned_hi, b + db, NSTEP, j + 1)
                            dve.tensor_tensor(pT_lo[j % TSLOTS][:, 0:w], banks[:, T_BANK + j % 2, 0:w],
                                              pT_hi[j % TSLOTS][:, 0:w].bitcast(F32), ALU.subtract)\
                                .then_inc(turned_lo, 1)
                        elif kind == "out":
                            wait(dve, out_hi, b + db, NG, j + 1)
                            cs = slice(256 * j, 256 * j + WIDTH[j])
                            dve.tensor_tensor(oT_lo[:, cs], banks[:, O_BANK, 0:WIDTH[j]], oT_hi[:, cs].bitcast(F32),
                                              ALU.subtract).then_inc(out_lo, 1)
                        elif kind == "prep":
                            src = banks[:, MISC, 0:512]
                            if j < 3:
                                wait(dve, prep_hi, b + db, PREP, j + 1)
                                w = min(512, SKP - 512 * j)
                                if j == 2:
                                    dve.tensor_tensor(ctxT_lo[i][:, 1024:1408], src[:, 0:384],
                                                      ctxT_hi[i][:, 1024:1408].bitcast(F32), ALU.subtract)
                                    dve.tensor_tensor(ctxT_lo[i][:, 1408:SKP], src[:, 384 + SHIFT:512],
                                                      ctxT_hi[i][:, 1408:SKP].bitcast(F32), ALU.subtract)\
                                        .then_inc(prep_read, 1)
                                else:
                                    dve.tensor_tensor(ctxT_lo[i][:, 512 * j:512 * j + w], src[:, 0:w],
                                                      ctxT_hi[i][:, 512 * j:512 * j + w].bitcast(F32), ALU.subtract)\
                                        .then_inc(prep_read, 1)
                            else:
                                wait(dve, prep_ready, b + db, PREP, j + 1)
                                n = j - 3
                                wait(dve, q_split, b + db, 4, n)
                                dve.tensor_tensor(qf[:, :, :], src[:, 0:4 * S].rearrange("p (h q) -> p h q", h=4),
                                                  u[:, 4 * n:4 * n + 4].unsqueeze(2).to_broadcast([128, 4, S]),
                                                  ALU.add).then_inc(prep_read, 1)
                        elif kind == "project":
                            wait(dve, proj_ready, b + db, 1, 1)
                            wait(dve, x1_in[i], b + db, 8, 8 if i else 16)
                            dve.tensor_tensor(x2[i][:, :], banks[0:S, MISC, 0:D], x1[i][:, :], ALU.add)\
                                .then_inc(x2_ready, 1)

                periods(dve, emit)

            @block.tensor
            def _(pe):
                pe.wait_ge(zeroed, 2 * 3 + 1)

                def score(b, i, n):
                    t, half = n // 2, n % 2
                    rows = slice(t * 128, (t + 1) * 128)
                    if n == 0:
                        wait(pe, q_split, b, 4, 4)
                        wait(pe, prep_read, b, PREP, PREP)
                    wait(pe, scores_taken, b, 2 * NT, n - 1)
                    for qpart, kparts in ((qh[i], (ctxT_hi[i], ctxT_lo[i])), (ql[i], (ctxT_hi[i],))):
                        for kpart in kparts:
                            first = qpart is qh[i] and kpart is ctxT_hi[i]
                            for c in (2 * half, 2 * half + 1):
                                last = pe.matmul(banks[:, S_BANK + c, 0:CW], qpart[:, rows],
                                                 kpart[:, c * CW:(c + 1) * CW], start=first, stop=qpart is ql[i])
                    last.then_inc(scores_ready, 1)

                def turn(b, j):
                    g, k0 = STEPS[j]
                    if k0 == 0:
                        wait(pe, probs_ready, b, NT, tiles_of(g)[-1] + 1)
                    wait(pe, turned_lo, b, NSTEP, j - 1)
                    for kk in range(KPB[g]):
                        k = k0 + kk
                        c0 = k * 128 if k < KT - 1 else SKP - 128
                        for n, t in enumerate(tiles_of(g)):
                            r = rows_of(t)
                            at_col = kk * WIDTH[g] + n * 128
                            last = pe.transpose(banks[:, T_BANK + j % 2, at_col:at_col + r],
                                                prob(t)[0:r, c0:c0 + 128], ident[0:r, 0:r])
                    last.then_inc(turned, 1)

                def values(b, i, j):
                    g, k0 = STEPS[j]
                    w = WIDTH[g]
                    wait(pe, turned_lo, b, NSTEP, j + 1)
                    if k0 == 0:
                        wait(pe, out_lo, b, NG, g)
                        if g == 0:
                            wait(pe, ctx_split, b, 3, 3)
                    for kk in range(KPB[g]):
                        k = k0 + kk
                        cs = slice(kk * w, (kk + 1) * w)
                        for stationary, moving in ((ctx_hi[i], pT_hi), (ctx_hi[i], pT_lo), (ctx_lo[i], pT_hi)):
                            last = pe.matmul(banks[:, O_BANK, 0:w], stationary[:, k, :], moving[j % TSLOTS][:, cs],
                                             start=(k == 0 and stationary is ctx_hi[i] and moving is pT_hi),
                                             stop=(k == KT - 1 and stationary is ctx_lo[i]))
                    last.then_inc(values_done, 1)
                    return last

                def prep(b, i, r):
                    wait(pe, prep_read, b, PREP, r)
                    wait(pe, x2_ready, b, 1, -1)
                    if r < 3:
                        if r == 0:
                            wait(pe, nat_in, b, 32, 32)
                        for n in range(4):
                            last = pe.transpose(banks[:, MISC, n * 128:(n + 1) * 128], nat[:, 4 * r + n, :], ident[:, :])
                    else:
                        if r == 3:
                            wait(pe, rows_in[i], b, 16, 16 if i else 32)
                        for n in range(4):
                            h = 4 * (r - 3) + n
                            dst = banks[:, MISC, n * S:(n + 1) * S]
                            pe.matmul(dst, A_hi[:, h, :], n2h[i][:, :], start=True, stop=False)
                            pe.matmul(dst, A_hi[:, h, :], n2l[i][:, :], start=False, stop=False)
                            last = pe.matmul(dst, A_lo[:, h, :], n2h[i][:, :], start=False, stop=True)
                    last.then_inc(prep_ready, 1)

                def project(b):
                    wait(pe, out_lo, b, NG, NG)
                    if known(b):
                        pe.wait_ge(prep_read, min(PREP * (b + 2), PREP * NB))
                    else:
                        wait(pe, prep_read, b, PREP, 2 * PREP)
                    dst = banks[0:S, MISC, 0:D]
                    for h in range(H):
                        oh, ol = oT_hi[:, h:S * H:H], oT_lo[:, h:S * H:H]
                        pe.matmul(dst, oh, VO_hi[:, h, :], start=(h == 0), stop=False)
                        pe.matmul(dst, oh, VO_lo[:, h, :], start=False, stop=False)
                        last = pe.matmul(dst, ol, VO_hi[:, h, :], start=False, stop=(h == H - 1))
                    last.then_inc(proj_ready, 1)

                LAG = 2

                def emit(b, odd):
                    for _, kind, db, j in ORDER:
                        if kind == "step":
                            if here(b, db):
                                turn(b + db, j)
                            jj, dd = (j - LAG, db) if j >= LAG else (j - LAG + NSTEP, db - 1)
                            if here(b, dd):
                                last = values(b + dd, odd if dd % 2 == 0 else 1 - odd, jj)
                        elif not here(b, db):
                            continue
                        elif kind == "score":
                            score(b + db, odd, j)
                        elif kind == "prep":
                            prep(b + db, 1 - odd, j)
                        elif kind == "project":
                            project(b + db)

                periods(pe, emit)


TT = (NTOK + 127) // 128
TPAD = TT * 128
TG = [slice(4 * g, min(4 * g + 4, TT)) for g in range((TT + 3) // 4)]
NTG = len(TG)
LASTROWS = NTOK - (TT - 1) * 128
CT = 400
UNITS = [(m, c) for m in range(HID // 128) for c in range(NTOK // CT)]
NU = len(UNITS)


def experts(nc, Wg, W1, b1, W11, b11, W2, b2, Ws1, bs1, Ws11, bs11, Ws2, bs2,
            banks, ident, x2_dram, out):
    with ExitStack() as ctx:
        def sb(name, shape, dt=F32):
            return ctx.enter_context(nc.sbuf_tensor(name, shape, dt))

        def sem(name):
            return ctx.enter_context(nc.semaphore(name))

        def pair(name, shape, dt=F32):
            return [sb(f"{name}{i}", shape, dt) for i in range(2)]

        y = sb("y", [128, TT, D])
        cen3, nrm3 = sb("cen3", [128, TT, D]), sb("nrm3", [128, TT, D])
        sq3 = sb("sq3", [128, 4, D])
        st3 = sb("st3", [128, 5, TT])
        t_hi, t_lo = sb("t_hi", [128, TPAD], F32R), sb("t_lo", [128, TPAD], F32R)
        wg, wg_hi, wg_lo = sb("wg", [128, NE]), sb("wg_hi", [128, NE], F32R), sb("wg_lo", [128, NE], F32R)
        b_rows, b_cols = sb("b_rows", [2 * NX, 2, 128]), sb("b_cols", [128, 2, 2 * NX])
        b2_rows = sb("b2_rows", [NE + 1, D])
        logits = sb("logits", [128, TT, NE])
        order16 = sb("order16", [128, NE])
        rank = sb("rank", [128, TT, NE])
        top = sb("top", [128, 6, TT])
        pick = [sb(f"pick{i}", [128, TT, NE]) for i in range(2)]
        gates = sb("gates", [128, TT, NX])
        gatesT = sb("gatesT", [NE + 1, TT, 128])
        w_raw = pair("w_raw", [128, 3, HID])
        w_hi, w_lo = pair("w_hi", [128, 3, HID], F32R), pair("w_lo", [128, 3, HID], F32R)
        act_out, hid = pair("act_out", [128, CT]), pair("hid", [128, CT])
        h_hi, h_lo = pair("h_hi", [128, 2, TPAD], F32R), pair("h_lo", [128, 2, TPAD], F32R)

        e_x_in, e_small_in, w_in = sem("e_x_in"), sem("e_small_in"), [sem("w_in0"), sem("w_in1")]
        passed_act = sem("passed_act")
        e_consts, e_padded = sem("e_consts"), sem("e_padded")
        e_chain, e_pool_chain = sem("e_chain"), sem("e_pool_chain")
        e_var, e_std, e_normed = sem("e_var"), sem("e_std"), sem("e_normed")
        tT_ready, tT_hi, tT_lo = sem("tT_ready"), sem("tT_hi"), sem("tT_lo")
        wg_split = sem("wg_split")
        b_ready, b_copied = sem("b_ready"), sem("b_copied")
        l_ready = sem("l_ready")
        g_diff, g_exp, g_done = sem("g_diff"), sem("g_exp"), sem("g_done")
        gT_ready, gT_copied = sem("gT_ready"), sem("gT_copied")
        yb_ready = sem("yb_ready")
        whi_made, w_split = sem("whi_made"), sem("w_split")
        ab_ready, silu_done, hid_done = sem("ab_ready"), sem("silu_done"), sem("hid_done")
        hhi_done, hlo_done = sem("hhi_done"), sem("hlo_done")
        ye_ready, y_added = sem("ye_ready"), sem("y_added")
        e_stored = sem("e_stored")

        def known(e):
            return isinstance(e, int)

        def wait(engine, sem, e, per, plus):
            if not known(e) or e * per + plus > 0:
                engine.wait_ge(sem, at(e, per, plus))

        def bank(n, rows=128, width=512, a=None):
            p = banks[0:rows, n, 0:width]
            return p if a is None else p.rearrange("p (a n) -> p a n", a=a)

        def tcols(g):
            return slice(TG[g].start * 128, TG[g].stop * 128)

        def ntiles(g):
            return TG[g].stop - TG[g].start

        def turns(engine, emit):
            emit(0, 0)
            with engine.Fori(1, NX - 2, 2) as e:
                emit(e, 1)
                emit(e + 1, 0)
            emit(NX - 1, 1)
            emit(NX, 0)

        with nc.Block() as block:
            @block.sync
            def _(sp):
                for g in range(NTG - 1):
                    sp.dma_start(y[:, TG[g], :], x2_dram[tcols(g), :].rearrange("(t p) d -> p t d", p=128))\
                        .then_inc(e_x_in, 16)
                sp.dma_start(y[0:LASTROWS, TT - 1, :], x2_dram[(TT - 1) * 128:NTOK, :]).then_inc(e_x_in, 16)

                def load(e, odd, a, b, c):
                    wait(sp, w_split, e, 1, -1)
                    for n, w in enumerate((a, b)):
                        sp.dma_start(w_raw[odd][:, n, :], w).then_inc(w_in[odd], 16)
                    sp.dma_start(w_raw[odd][:, 2, :].rearrange("p (m d) -> p m d", m=2),
                                 c.rearrange("(m p) d -> p m d", p=128)).then_inc(w_in[odd], 16)

                load(0, 0, W1[0], W11[0], W2[0])
                load(1, 1, W1[1], W11[1], W2[1])
                with sp.Fori(2, NE - 1, 2) as e:
                    for odd in range(2):
                        one = bass.ds(e + odd, 1)
                        load(e + odd, odd, *(w[one].rearrange("a k d -> (a k) d") for w in (W1, W11, W2)))
                for n in range(2):
                    cs = slice(n * HID, (n + 1) * HID)
                    load(NE + n, n, Ws1[:, cs], Ws11[:, cs], Ws2[cs, :])
                for g in range(NTG):
                    wait(sp, y_added, NX, NTG, g + 1)
                    if g < NTG - 1:
                        sp.dma_start(out[tcols(g), :].rearrange("(t p) d -> p t d", p=128), y[:, TG[g], :])\
                            .then_inc(e_stored, 16)
                    else:
                        sp.dma_start(out[(TT - 1) * 128:NTOK, :], y[0:LASTROWS, TT - 1, :]).then_inc(e_stored, 16)
                sp.wait_ge(e_stored, 16 * NTG)

            @block.gpsimd
            def _(pool):
                for n in range(NE):
                    pool.memset(order16[:, n:n + 1], float(NE - n)).then_inc(e_consts, 1)
                pool.memset(gates[:, :, NE:NX], 1.0).then_inc(e_consts, 1)
                for i in range(2):
                    for t in (h_hi, h_lo):
                        pool.memset(t[i][:, :, NTOK:TPAD].bitcast(F32), 0.0).then_inc(e_padded, 1)
                pool.wait_ge(e_padded, 4)

                def emit(e, odd):
                    if known(e) and e == NX:
                        return
                    for n, (m, c) in enumerate(UNITS):
                        wait(pool, hhi_done, e, NU, n + 1)
                        cs = slice(c * CT, (c + 1) * CT)
                        pool.tensor_tensor(h_lo[odd][:, m, cs], hid[n % 2][:, :], h_hi[odd][:, m, cs].bitcast(F32),
                                           ALU.subtract).then_inc(hlo_done, 1)

                turns(pool, emit)

            @block.scalar
            def _(act):
                act.dma_start(wg[:, :], Wg).then_inc(e_small_in, 16)
                for n, (routed, shared) in enumerate(((b1, bs1), (b11, bs11))):
                    act.dma_start(b_rows[0:2 * NE, n, :], routed.rearrange("e (m p) -> (e m) p", p=128))\
                        .then_inc(e_small_in, 16)
                    act.dma_start(b_rows[2 * NE:2 * NX, n, :], shared.rearrange("(m p) -> m p", p=128))\
                        .then_inc(e_small_in, 16)
                act.dma_start(b2_rows[0:NE, :], b2).then_inc(e_small_in, 16)
                act.dma_start(b2_rows[NE:NE + 1, :], bs2.rearrange("(a d) -> a d", a=1)).then_inc(e_small_in, 16)
                for g in range(NTG):
                    act.wait_ge(e_var, g + 1)
                    act.activation(st3[:, 3, TG[g]], st3[:, 2, TG[g]], ACT.Sqrt).then_inc(e_std, 1)

                def split(e, odd):
                    wait(act, w_in[odd], e, 24, 24 + (24 if odd == 0 else 0))
                    wait(act, ye_ready, e, NTG, -NTG)
                    act.copy(w_hi[odd][:, :, :], w_raw[odd][:, :, :]).then_inc(whi_made, 1)

                for g in range(NTG):
                    act.wait_ge(tT_ready, g + 1)
                    act.copy(t_hi[:, tcols(g)], bank(g, width=128 * ntiles(g))).then_inc(tT_hi, 1)
                split(0, 0)
                split(1, 1)
                act.wait_ge(b_ready, 1)
                act.copy(b_cols[:, :, :], bank(7, width=4 * NX, a=2)).then_inc(b_copied, 1)
                act.wait_ge(g_diff, 1)
                act.activation(top[:, 3, :], top[:, 2, :], ACT.Exp).then_inc(g_exp, 1)
                for g in range(NTG):
                    act.wait_ge(gT_ready, g + 1)
                    act.copy(gatesT[:, TG[g], :], bank(g, NE + 1, 128 * ntiles(g), a=ntiles(g))).then_inc(gT_copied, 1)

                def emit(e, odd):
                    if known(e) and e == NX:
                        return
                    for n in range(NU + 1):
                        if n < NU:
                            m, c = UNITS[n]
                            wait(act, hid_done, e, NU, n - 1)
                            wait_apart(act, ab_ready, e, NU, n + 1, passed_act)
                            j = 2 * e + m
                            bias = b_cols[:, 0, j:j + 1] if known(e) else b_cols[:, 0, bass.ds(j, 1)]
                            act.activation(act_out[n % 2][:, :], bank(2 * (n % 2), width=CT), ACT.Silu,
                                           bias=bias).then_inc(silu_done, 1)
                        if n:
                            m, c = UNITS[n - 1]
                            wait(act, hid_done, e, NU, n)
                            if n == 1:
                                wait(act, ye_ready, e, NTG, -NTG)
                            act.copy(h_hi[odd][:, m, c * CT:(c + 1) * CT], hid[(n - 1) % 2][:, :]).then_inc(hhi_done, 1)
                        if n == 5 and not (known(e) and (e == 0 or e + 1 >= NX)):
                            split(e + 1, 1 - odd)

                turns(act, emit)

            @block.vector
            def _(dve):
                link = Chain(dve, e_chain)
                dve.memset(y[LASTROWS:128, TT - 1, :], 0.0)
                dve.wait_ge(e_x_in, 16 * NTG)
                dve.wait_ge(e_small_in, 16 * 7)
                link(dve.tensor_copy(wg_hi[:, :], wg[:, :]))
                dve.tensor_tensor(wg_lo[:, :], wg[:, :], wg_hi[:, :].bitcast(F32), ALU.subtract).then_inc(wg_split, 1)
                for g in range(NTG):
                    ts, n = TG[g], ntiles(g)
                    wide = [128, n, D]
                    link(dve.tensor_reduce(st3[:, 0, ts], y[:, ts, :], AX.X, ALU.add))
                    link(dve.tensor_scalar(st3[:, 1, ts], st3[:, 0, ts], 1.0 / D, None, ALU.mult))
                    link(dve.tensor_tensor(cen3[:, ts, :], y[:, ts, :],
                                           st3[:, 1, ts].unsqueeze(2).to_broadcast(wide), ALU.subtract))
                    link(dve.tensor_tensor(sq3[:, 0:n, :], cen3[:, ts, :], cen3[:, ts, :], ALU.mult))
                    link(dve.tensor_reduce(st3[:, 0, ts], sq3[:, 0:n, :], AX.X, ALU.add))
                    dve.tensor_scalar(st3[:, 2, ts], st3[:, 0, ts], 1.0 / D, EPS, ALU.mult, ALU.add).then_inc(e_var, 1)
                for g in range(NTG):
                    ts = TG[g]
                    dve.wait_ge(e_std, g + 1)
                    link(dve.reciprocal(st3[:, 4, ts], st3[:, 3, ts]))
                    dve.tensor_tensor(nrm3[:, ts, :], cen3[:, ts, :],
                                      st3[:, 4, ts].unsqueeze(2).to_broadcast([128, ntiles(g), D]), ALU.mult)\
                        .then_inc(e_normed, 1)
                for g in range(NTG):
                    dve.wait_ge(tT_hi, g + 1)
                    dve.tensor_tensor(t_lo[:, tcols(g)], bank(g, width=128 * ntiles(g)), t_hi[:, tcols(g)].bitcast(F32),
                                      ALU.subtract).then_inc(tT_lo, 1)

                def split(e, odd):
                    wait(dve, whi_made, e, 1, 1)
                    dve.tensor_tensor(w_lo[odd][:, :, :], w_raw[odd][:, :, :], w_hi[odd][:, :, :].bitcast(F32),
                                      ALU.subtract).then_inc(w_split, 1)

                dve.wait_ge(l_ready, 1)
                dve.wait_ge(e_consts, NE + 1)
                wide = [128, TT, NE]
                falling = order16[:, :].unsqueeze(1).to_broadcast(wide)
                link(dve.tensor_copy(logits[:, :, :], bank(4, width=TT * NE, a=TT)))
                for n in range(2):
                    link(dve.tensor_reduce(top[:, n, :], logits[:, :, :], AX.X, ALU.max))
                    link(dve.tensor_tensor(rank[:, :, :], logits[:, :, :],
                                           top[:, n, :].unsqueeze(2).to_broadcast(wide), ALU.is_equal))
                    link(dve.tensor_tensor(rank[:, :, :], rank[:, :, :], falling, ALU.mult))
                    link(dve.tensor_reduce(top[:, 4, :], rank[:, :, :], AX.X, ALU.max))
                    link(dve.tensor_tensor(pick[n][:, :, :], rank[:, :, :],
                                           top[:, 4, :].unsqueeze(2).to_broadcast(wide), ALU.is_equal))
                    if n == 0:
                        link(dve.scalar_tensor_tensor(logits[:, :, :].rearrange("p t e -> p (t e)"),
                                                      pick[0][:, :, :].rearrange("p t e -> p (t e)"), -3e38,
                                                      logits[:, :, :].rearrange("p t e -> p (t e)"),
                                                      ALU.mult, ALU.add))
                dve.tensor_tensor(top[:, 2, :], top[:, 1, :], top[:, 0, :], ALU.subtract).then_inc(g_diff, 1)
                split(0, 0)
                split(1, 1)
                dve.wait_ge(g_exp, 1)
                link(dve.tensor_scalar(top[:, 4, :], top[:, 3, :], 1.0, None, ALU.add))
                link(dve.reciprocal(top[:, 5, :], top[:, 4, :]))
                link(dve.tensor_tensor(pick[1][:, :, :], pick[1][:, :, :],
                                       top[:, 3, :].unsqueeze(2).to_broadcast(wide), ALU.mult))
                link(dve.tensor_tensor(pick[0][:, :, :], pick[0][:, :, :], pick[1][:, :, :], ALU.add))
                dve.tensor_tensor(gates[:, :, 0:NE], pick[0][:, :, :],
                                  top[:, 5, :].unsqueeze(2).to_broadcast(wide), ALU.mult).then_inc(g_done, 1)
                for g in range(NTG):
                    ts, n = TG[g], ntiles(g)
                    dve.wait_ge(yb_ready, g + 1)
                    dve.tensor_tensor(y[:, ts, :], bank(4 + g, width=128 * n, a=n), y[:, ts, :], ALU.add)\
                        .then_inc(y_added, 1)
                dve.wait_ge(b_copied, 1)
                dve.wait_ge(g_done, 1)

                def emit(e, odd):
                    def add(g):
                        prev = e - 1
                        wait(dve, ye_ready, prev, NTG, g + 1)
                        wait(dve, y_added, prev, NTG, g + 1)
                        for i in range(ntiles(g)):
                            t = TG[g].start + i
                            gate = gates[:, t, prev:prev + 1] if known(e) else gates[:, t, bass.ds(prev, 1)]
                            last = dve.scalar_tensor_tensor(y[:, t, :], bank(4 + g)[:, i * D:(i + 1) * D], gate,
                                                            y[:, t, :], ALU.mult, ALU.add)
                        last.then_inc(y_added, 1)

                    for n in range(NU):
                        m, c = UNITS[n]
                        if not (known(e) and e == NX):
                            wait(dve, silu_done, e, NU, n + 1)
                            wait(dve, hlo_done, e, NU, n - 1)
                            j = 2 * e + m
                            bias = b_cols[:, 1, j:j + 1] if known(e) else b_cols[:, 1, bass.ds(j, 1)]
                            dve.scalar_tensor_tensor(hid[n % 2][:, :], bank(2 * (n % 2) + 1, width=CT), bias,
                                                     act_out[n % 2][:, :], ALU.add, ALU.mult).then_inc(hid_done, 1)
                        if n % 2 and not (known(e) and e == 0):
                            add(n // 2)
                        if n == 6 and not (known(e) and (e == 0 or e + 1 >= NX)):
                            split(e + 1, 1 - odd)

                turns(dve, emit)

            @block.tensor
            def _(pe):
                for g in range(NTG):
                    pe.wait_ge(e_normed, g + 1)
                    for i in range(ntiles(g)):
                        last = pe.transpose(bank(g)[:, i * 128:(i + 1) * 128], nrm3[:, TG[g].start + i, :], ident[:, :])
                    last.then_inc(tT_ready, 1)
                pe.wait_ge(e_small_in, 16 * 7)
                for n in range(2):
                    last = pe.transpose(bank(7)[:, n * 2 * NX:(n + 1) * 2 * NX], b_rows[:, n, :],
                                        ident[0:2 * NX, 0:2 * NX])
                last.then_inc(b_ready, 1)
                pe.wait_ge(wg_split, 1)
                for g in range(NTG):
                    pe.wait_ge(tT_lo, g + 1)
                    for t in range(TG[g].start, TG[g].stop):
                        dst = bank(4)[:, t * NE:(t + 1) * NE]
                        cs = slice(t * 128, (t + 1) * 128)
                        pe.matmul(dst, t_hi[:, cs], wg_hi[:, :], start=True, stop=False)
                        pe.matmul(dst, t_hi[:, cs], wg_lo[:, :], start=False, stop=False)
                        last = pe.matmul(dst, t_lo[:, cs], wg_hi[:, :], start=False, stop=True)
                last.then_inc(l_ready, 1)
                pe.wait_ge(g_done, 1)
                for g in range(NTG):
                    for i in range(ntiles(g)):
                        last = pe.transpose(bank(g, NE + 1)[:, i * 128:(i + 1) * 128],
                                            gates[:, TG[g].start + i, 0:NE + 1], ident[:, :])
                    last.then_inc(gT_ready, 1)
                pe.wait_ge(b_copied, 1)
                for g in range(NTG):
                    pe.wait_ge(gT_copied, g + 1)
                    for i in range(ntiles(g)):
                        last = pe.matmul(bank(4 + g)[:, i * D:(i + 1) * D], gatesT[:, TG[g].start + i, :],
                                         b2_rows[:, :], start=True, stop=True)
                    last.then_inc(yb_ready, 1)
                pe.wait_ge(e_padded, 4)

                def emit(e, odd):
                    def unit(n):
                        m, c = UNITS[n]
                        if n == 0:
                            wait(pe, w_split, e, 1, 1)
                        wait(pe, silu_done, e, NU, n - 1)
                        wait(pe, hid_done, e, NU, n - 1)
                        ts, ms = slice(c * CT, (c + 1) * CT), slice(m * 128, (m + 1) * 128)
                        for k in range(2):
                            dst = bank(2 * (n % 2) + k, width=CT)
                            pe.matmul(dst, w_hi[odd][:, k, ms], t_hi[:, ts], start=True, stop=False)
                            pe.matmul(dst, w_hi[odd][:, k, ms], t_lo[:, ts], start=False, stop=False)
                            last = pe.matmul(dst, w_lo[odd][:, k, ms], t_hi[:, ts], start=False, stop=True)
                        last.then_inc(ab_ready, 1)

                    def down(g):
                        prev, p = e - 1, 1 - odd
                        if g == 0:
                            wait(pe, hlo_done, prev, NU, NU)
                        wait(pe, y_added, prev, NTG, g + 1)
                        for i in range(ntiles(g)):
                            dst = bank(4 + g)[:, i * D:(i + 1) * D]
                            cs = slice((TG[g].start + i) * 128, (TG[g].start + i + 1) * 128)
                            for m in range(2):
                                w = slice(m * D, (m + 1) * D)
                                pe.matmul(dst, h_hi[p][:, m, cs], w_hi[p][:, 2, w], start=(m == 0), stop=False)
                                pe.matmul(dst, h_hi[p][:, m, cs], w_lo[p][:, 2, w], start=False, stop=False)
                                last = pe.matmul(dst, h_lo[p][:, m, cs], w_hi[p][:, 2, w], start=False, stop=(m == 1))
                        last.then_inc(ye_ready, 1)

                    for n in range(NU):
                        if not (known(e) and e == NX):
                            unit(n)
                        if n % 2 and not (known(e) and e == 0):
                            down(n // 2)

                turns(pe, emit)


_INS = ["x", "ctx_1024", "mask_BxSxS2_bk1", "L0_attn_WQ", "L0_attn_WK", "L0_attn_WV",
        "L0_xattn_W_Q", "L0_xattn_b_Q", "L0_xattn_W_K", "L0_xattn_b_K", "L0_xattn_W_V", "L0_xattn_b_V",
        "L0_xattn_W_out", "L0_xattn_b_out",
        "L0_ffn_Wg", "L0_ffn_W1", "L0_ffn_b1", "L0_ffn_W11", "L0_ffn_b11", "L0_ffn_W2", "L0_ffn_b2",
        "L0_ffn_Ws1", "L0_ffn_bs1", "L0_ffn_Ws11", "L0_ffn_bs11", "L0_ffn_Ws2", "L0_ffn_bs2"]


def kernel(**inputs):
    import numpy as _np
    import concourse.bacc as _bacc
    from concourse import mybir as _mybir
    from concourse.bass_utils import run_bass_kernel_spmd as _run

    nc = _bacc.Bacc("TRN2", target_bir_lowering=False, num_devices=1)
    arrays, args = {}, []
    for name in _INS:
        a = _np.ascontiguousarray(inputs[name])
        arrays[f"in_{name}"] = a
        args.append(nc.dram_tensor(f"in_{name}", a.shape, _mybir.dt.from_np(a.dtype), kind="ExternalInput").ap())
    res = nc.dram_tensor("out_0", (NTOK, D), F32, kind="ExternalOutput").ap()
    decoder(nc, *args, res)
    r = _run(nc, [arrays], core_ids=[0])
    return r.results[0]["out_0"].reshape(NB, S, D)
```

```python
from contextlib import ExitStack

import concourse.bass as bass
from concourse import mybir

F32 = mybir.dt.float32
F32R = mybir.dt.float32r
U8 = mybir.dt.uint8
ALU = mybir.AluOpType
ACT = mybir.ActivationFunctionType
AX = mybir.AxisListType

NB, S, D = 16, 100, 128
SK = 1444
H, DK = 16, 64
NE, HID = 16, 256
NX = NE + 2
NTOK = NB * S
EPS = 1e-5
BAND = 64
LOWER, UPPER = BAND // 2, (BAND - 1) // 2
MASKED = -1e30
PAD = -3e38

CB = 4
NC = NB // CB

KT = 12
LASTK = SK - 11 * 128
SHIFT = 128 - LASTK - 4
CW = 362
SKP = 4 * CW
FT = 12
NT = FT + 1
QR = 128 // H
HALF = 64
NG = 6
WIDTH = [256] * 5 + [320]
KPB = [2] * 5 + [1]
STEPS = [(g, k) for g in range(NG) for k in range(0, KT, KPB[g])]
NSTEP = len(STEPS)
PSLOTS = 6
TSLOTS = 4
MSLOTS = 3
PREP = 7


def tiles_of(g):
    return [2 * g, 2 * g + 1] + ([FT] if g == NG - 1 else [])


def rows_of(t):
    return 128 if t < FT else HALF


def group_of(t):
    return min(t // 2, NG - 1)


def steps_to(g):
    return sum(gg <= g for gg, _ in STEPS)


def period():
    split = 27
    steps = [("step", -1, j) for j in range(split, NSTEP)] + [("step", 0, j) for j in range(split)]
    cost = [1.28 if STEPS[j][0] == NG - 1 else 2.05 for _, _, j in steps]
    total, at, out = sum(cost), 0.0, []
    for c, (kind, db, j) in zip(cost, steps):
        out.append(((at + c / 2) / total, kind, db, j))
        at += c
    for n in range(2 * NT):
        out.append(((n + 0.5) / (2 * NT), "score", 0, n))
    out.append((0.41, "project", -1, 0))
    for r, at in enumerate((0.5, 0.573, 0.646, 0.719, 0.792, 0.865, 0.938)):
        out.append((at, "prep", 1, r))
    out.sort()
    return [(n, kind, db, j) for n, (_, kind, db, j) in enumerate(out)]


ORDER = period()
LENGTH = len(ORDER)
LAG = 3


def lagged(j, db):
    return (j - LAG, db) if j >= LAG else (j - LAG + NSTEP, db - 1)


def ends_group(j, db):
    jj, dd = lagged(j, db)
    g, k0 = STEPS[jj]
    return (dd, g) if k0 + KPB[g] == KT else None


def shared_banks():
    rounds, groups = {}, {}
    last, current = ("prep", 0, PREP - 1), None
    for turn in range(2):
        for _, kind, db, j in ORDER:
            if kind == "step":
                jj, dd = lagged(j, db)
                g, k0 = STEPS[jj]
                current = (g, dd)
                if k0 == 0:
                    groups[g] = (*last[:1], last[1] - dd, last[2])
            elif kind in ("prep", "project"):
                rounds[kind, j] = current
                last = (kind, db, j)
        last, current = (last[0], last[1] - 1, last[2]), (current[0], current[1] - 1)
    return rounds, groups


ROUNDS, GROUPS = shared_banks()


def later(items):
    out = []
    for at, kind, db, j in items:
        out.append((at - LENGTH, kind, db - 1, j) if at >= LENGTH else (at, kind, db, j))
    return sorted(out)


def act_order():
    out = []
    for n, kind, db, j in ORDER:
        if kind == "score" and j % 2:
            out.append((n + 1.5, "exp", db, j // 2))
        elif kind == "step":
            out.append((n + 0.1, "step", db, j))
            if ends_group(j, db):
                out.append((n + 0.05, "out", *ends_group(j, db)))
        elif kind == "prep":
            out.append((n + 0.3, "prep", db, j))
    return later(out)


def dve_order():
    out = []
    for n, kind, db, j in ORDER:
        if kind == "score":
            out.append((n + 0.2, "score", db, j))
            if j % 2:
                out.append((n + 3.6, "recip", db, j // 2))
        elif kind == "step":
            out.append((n + 1.1, "step", db, j))
            if ends_group(j, db):
                out.append((n + 1.05, "out", *ends_group(j, db)))
        elif kind == "prep":
            out.append((n + 0.9, "prep", db, j))
        elif kind == "project":
            out.append((n + 0.9, "project", db, j))
    return later(out)


def pool_order():
    out = []
    for n, kind, db, j in ORDER:
        if kind == "score" and j % 2 == 0:
            t = j // 2 + 1
            out.append((n + 0.5, "bias", db if t < NT else db + 1, t % NT))
        if kind == "score" and j % 2:
            out.append((n + 4.6, "norm", db, j // 2))
        elif kind == "prep" and j >= 3:
            out.append((n + 1.6, "prep", db, j))
    for n in range(3):
        out.append(((0.42 + 0.08 * n) * LENGTH, "split", 1, n))
    return later(out)


def wait_apart(engine, sem, b, per, plus, passed):
    if not isinstance(b, int) or b * per + plus > 0:
        engine.wait_ge(sem, at(b, per, plus))
        if not isinstance(b, int):
            engine.sem_inc(passed, 1)


def at(b, per, plus):
    return b * per + plus


def decoder(nc, x, ctx_in, mask, wq_s, wk_s, wv_s, W_Q, b_Q, W_K, b_K, W_V, b_V, W_out, b_out,
            Wg, W1, b1, W11, b11, W2, b2, Ws1, bs1, Ws11, bs11, Ws2, bs2, out):
    with ExitStack() as whole:
        def psum_banks(n, name):
            return whole.enter_context(nc.psum_tensor(name, [128, n, 512], F32))

        def keep(name, shape, dt=F32):
            return whole.enter_context(nc.sbuf_tensor(name, shape, dt))

        banks = psum_banks(8, "banks")
        ident = keep("ident", [128, 128])
        A_hi, A_lo = keep("A_hi", [128, H, D], F32R), keep("A_lo", [128, H, D], F32R)
        VO = keep("VO", [128, H, 2, D], F32R)
        u = keep("u", [128, H])
        c_all = keep("c_all", [128, NB, NT])
        x1_dram = nc.dram_tensor("x1_dram", (NB, S, D), F32, kind="Internal").ap()
        n2hi_dram = nc.dram_tensor("n2hi_dram", (NB, D, S), F32, kind="Internal").ap()
        n2lo_dram = nc.dram_tensor("n2lo_dram", (NB, D, S), F32, kind="Internal").ap()
        x2_dram = nc.dram_tensor("x2_dram", (NTOK, D), F32, kind="Internal").ap()

        self_attention(nc, x, wq_s, wk_s, wv_s, W_Q, b_Q, W_K, b_K, W_V, b_V, W_out, b_out,
                       banks, ident, A_hi, A_lo, VO, u, c_all,
                       x1_dram, n2hi_dram, n2lo_dram)
        cross_attention(nc, ctx_in, mask, banks, ident, A_hi, A_lo, VO, u, c_all,
                        x1_dram, n2hi_dram, n2lo_dram, x2_dram)
        experts(nc, Wg, W1, b1, W11, b11, W2, b2, Ws1, bs1, Ws11, bs11, Ws2, bs2,
                banks, ident, x2_dram, out)


class Chain:

    def __init__(self, engine, sem):
        self.engine, self.sem, self.count = engine, sem, 0

    def __call__(self, ins):
        ins.then_inc(self.sem, 1)
        self.count += 1
        self.engine.wait_ge(self.sem, self.count)


def self_attention(nc, x, wq_s, wk_s, wv_s, W_Q, b_Q, W_K, b_K, W_V, b_V, W_out, b_out,
                   banks, ident, A_hi, A_lo, VO, u, c_all,
                   x1_dram, n2hi_dram, n2lo_dram):
    with ExitStack() as ctx:
        def sb(name, shape, dt=F32):
            return ctx.enter_context(nc.sbuf_tensor(name, shape, dt))

        def sem(name):
            return ctx.enter_context(nc.semaphore(name))

        xt = sb("xt", [S, NB, D])
        cen, nrm = sb("cen", [S, NB, D]), sb("nrm", [S, NB, D])
        sq = sb("sq", [S, CB, D])
        st = sb("st", [S, 8, NB])
        xnT = sb("xnT", [128, NTOK])
        qT, kT = sb("qT", [128, NTOK]), sb("kT", [128, NTOK])
        v = sb("v", [S, NB, D])
        pr = sb("pr", [S, NB, S])
        prT = sb("prT", [S, NB, S])
        band = sb("band", [S, S])
        n2hi, n2lo = sb("n2hi", [128, NTOK], F32R), sb("n2lo", [128, NTOK], F32R)
        wsq, wsk, wsv = sb("wsq", [D, D]), sb("wsk", [D, D]), sb("wsv", [D, D])
        wQ, wK, wV = sb("wQ", [DK, H, D]), sb("wK", [DK, H, D]), sb("wV", [DK, H, D])
        wo = sb("wo", [D, H * DK])
        woT = sb("woT", [DK, H, D])
        bQ, bK, bV = sb("bQ", [DK, H]), sb("bK", [DK, H]), sb("bV", [DK, H])
        bo = sb("bo", [1, D])
        bVrep = sb("bVrep", [DK, H, S])
        bb = sb("bb", [DK, H])
        bbrep = sb("bbrep", [DK, QR, H])
        ones = sb("ones", [DK, S])
        wpad = sb("wpad", [128, 2 * 128 - H])
        kcol = sb("kcol", [128, 1])
        const_row = sb("const_row", [S, D])
        rmax, rsum, rinv = sb("rmax", [S, NB]), sb("rsum", [S, NB]), sb("rinv", [S, NB])

        x_in = [sem(f"x_in{c}") for c in range(NC)]
        wqk_in, wv_in = sem("wqk_in"), sem("wv_in")
        self_in = sem("self_in")
        consts = sem("consts")
        dve_chain, pool_chain = sem("dve_chain"), sem("pool_chain")
        squared, var_ready, std_ready = sem("squared"), sem("var_ready"), sem("std_ready")
        centered = sem("centered")
        normed = sem("normed")
        xT_ready, xT_copied = sem("xT_ready"), sem("xT_copied")
        q_ready, k_ready, v_ready = sem("q_ready"), sem("k_ready"), sem("v_ready")
        q_copied, k_copied, v_copied = sem("q_copied"), sem("k_copied"), sem("v_copied")
        s_ready, s_shifted, s_exp = sem("s_ready"), sem("s_shifted"), sem("s_exp")
        pT_ready, pT_copied = sem("pT_ready"), sem("pT_copied")
        o_ready, x1_ready = sem("o_ready"), sem("x1_ready")
        nT_ready, nT_hi, nT_lo = sem("nT_ready"), sem("nT_hi"), sem("nT_lo")
        w_ready, w_hi, w_done = sem("w_ready"), sem("w_hi"), sem("w_done")
        bias_made = sem("bias_made")
        stored = sem("stored")

        def cols(c):
            return slice(c * CB * S, (c + 1) * CB * S)

        def chunk(t, c):
            return t[:, c * CB:(c + 1) * CB, :]

        def bank(n, rows=128, width=512, a=None):
            p = banks[0:rows, n, 0:width]
            return p if a is None else p.rearrange("p (a n) -> p a n", a=a)

        def wbank(r):
            return 4 + r % 4

        R_SMALL, R_WOT, R_A, R_VO, R_CONST, R_C = 0, 1, 5, 9, 13, 14

        with nc.Block() as block:
            @block.sync
            def _(sp):
                for c in range(NC):
                    sp.dma_start(chunk(xt, c), x[c * CB:(c + 1) * CB].rearrange("b q d -> q b d"))\
                        .then_inc(x_in[c], 16)
                for t, w in ((wsq, wq_s), (wsk, wk_s), (wsv, wv_s)):
                    sp.dma_start(t[:, :], w).then_inc(self_in, 16)
                for c in range(NC):
                    sp.wait_ge(x1_ready, c + 1)
                    sp.dma_start(x1_dram[c * CB:(c + 1) * CB].rearrange("b q d -> q b d"), chunk(xt, c))\
                        .then_inc(stored, 16)
                    sp.wait_ge(nT_lo, c + 1)
                    for t, w in ((n2hi, n2hi_dram), (n2lo, n2lo_dram)):
                        sp.dma_start(w[c * CB:(c + 1) * CB].rearrange("b d q -> d b q"),
                                     t[:, cols(c)].bitcast(F32).rearrange("p (b q) -> p b q", b=CB))\
                            .then_inc(stored, 16)
                sp.wait_ge(stored, 16 * 3 * NC)

            @block.gpsimd
            def _(pool):
                link = Chain(pool, pool_chain)
                link(pool.memset(ident[:, :], 0.0))
                pool.affine_select(out=ident[:, :], in_=ident[:, :], compare_op=ALU.not_equal, fill=1.0,
                                   base=0, pattern=[[-1, 128]], channel_multiplier=1).then_inc(consts, 1)
                link(pool.memset(band[:, :], float(D) ** -0.5))
                link(pool.affine_select(out=band[:, :], in_=band[:, :], compare_op=ALU.is_ge, fill=0.0,
                                        base=LOWER, pattern=[[1, S]], channel_multiplier=-1))
                pool.affine_select(out=band[:, :], in_=band[:, :], compare_op=ALU.is_ge, fill=0.0,
                                   base=UPPER, pattern=[[-1, S]], channel_multiplier=1).then_inc(consts, 1)
                pool.memset(ones[:, :], 1.0).then_inc(consts, 1)
                pool.memset(wpad[:, :], 0.0).then_inc(consts, 1)
                pool.wait_ge(wqk_in, 16 * 4)
                link(pool.tensor_tensor(bb[:, :], bQ[:, :], bK[:, :], ALU.mult))
                pool.tensor_copy(bbrep[:, :, :], bb[:, :].unsqueeze(1).to_broadcast([DK, QR, H]))\
                    .then_inc(bias_made, 1)
                pool.wait_ge(wv_in, 16 * 4)
                pool.tensor_copy(bVrep[:, :, :], bV[:, :].unsqueeze(2).to_broadcast([DK, H, S]))\
                    .then_inc(bias_made, 1)

            @block.scalar
            def _(act):
                for t, w in ((wQ, W_Q), (wK, W_K)):
                    act.dma_start(t[:, :, :], w.rearrange("(h j) d -> j h d", j=DK)).then_inc(wqk_in, 16)
                for t, w in ((bQ, b_Q), (bK, b_K)):
                    act.dma_start(t[:, :], w.rearrange("(h j) -> j h", j=DK), allow_slow_non_contiguous=True).then_inc(wqk_in, 16)
                act.dma_start(wo[:, :], W_out).then_inc(wv_in, 16)
                act.dma_start(wV[:, :, :], W_V.rearrange("(h j) d -> j h d", j=DK)).then_inc(wv_in, 16)
                act.dma_start(bV[:, :], b_V.rearrange("(h j) -> j h", j=DK), allow_slow_non_contiguous=True).then_inc(wv_in, 16)
                act.dma_start(bo[:, :], b_out.rearrange("(a d) -> a d", a=1)).then_inc(wv_in, 16)

                def std(n):
                    act.wait_ge(var_ready, n + 1)
                    act.activation(st[:, 3, (n % NC) * CB:(n % NC + 1) * CB],
                                   st[:, 2, (n % NC) * CB:(n % NC + 1) * CB], ACT.Sqrt).then_inc(std_ready, 1)

                std(0)
                for c in range(NC):
                    if c + 1 < NC:
                        std(c + 1)
                    act.wait_ge(xT_ready, c + 1)
                    act.copy(xnT[:, cols(c)], bank(c, width=CB * S)).then_inc(xT_copied, 1)

                def split_hi(n, r, dst, scale=1.0):
                    act.wait_ge(w_ready, r + 1)
                    act.activation(dst[:, 4 * n:4 * n + 4, :], bank(wbank(r), a=4), ACT.Copy, scale=scale)\
                        .then_inc(w_hi, 1)

                for n in range(4):
                    split_hi(n, R_A + n, A_hi[:, :, :], 0.125)
                for n in range(4):
                    split_hi(n, R_VO + n, VO[:, :, 0, :])
                for c in range(NC):
                    act.wait_ge(q_ready, c + 1)
                    act.copy(qT[:, cols(c)], bank(c, width=CB * S)).then_inc(q_copied, 1)
                for c in range(NC):
                    act.wait_ge(v_ready, c + 1)
                    act.copy(chunk(v, c), bank(c, S, a=CB)).then_inc(v_copied, 1)
                for c in range(NC):
                    act.wait_ge(s_shifted, c + 1)
                    act.activation(chunk(pr, c), chunk(pr, c), ACT.Exp).then_inc(s_exp, 1)
                for c in range(NC):
                    act.wait_ge(pT_ready, c + 1)
                    act.copy(chunk(prT, c), bank(c, S, CB * S, a=CB)).then_inc(pT_copied, 1)
                for c in range(NC):
                    std(NC + c)
                for c in range(NC):
                    act.wait_ge(nT_ready, c + 1)
                    act.copy(n2hi[:, cols(c)], bank(c, width=CB * S)).then_inc(nT_hi, 1)

            @block.vector
            def _(dve):
                link = Chain(dve, dve_chain)

                def norm(c, n):
                    cs = slice(c * CB, (c + 1) * CB)
                    wide = [S, CB, D]
                    link(dve.tensor_reduce(st[:, 0, cs], chunk(xt, c), AX.X, ALU.add))
                    link(dve.tensor_scalar(st[:, 1, cs], st[:, 0, cs], 1.0 / D, None, ALU.mult))
                    link(dve.tensor_tensor(chunk(cen, c), chunk(xt, c),
                                           st[:, 1, cs].unsqueeze(2).to_broadcast(wide), ALU.subtract))
                    link(dve.tensor_tensor(sq[:, :, :], chunk(cen, c), chunk(cen, c), ALU.mult))
                    link(dve.tensor_reduce(st[:, 0, cs], sq[:, :, :], AX.X, ALU.add))
                    dve.tensor_scalar(st[:, 2, cs], st[:, 0, cs], 1.0 / D, EPS, ALU.mult, ALU.add)\
                        .then_inc(var_ready, 1)

                def scale(c, n):
                    cs = slice(c * CB, (c + 1) * CB)
                    dve.wait_ge(std_ready, n + 1)
                    link(dve.reciprocal(st[:, 4, cs], st[:, 3, cs]))
                    dve.tensor_tensor(chunk(nrm, c), chunk(cen, c),
                                      st[:, 4, cs].unsqueeze(2).to_broadcast([S, CB, D]), ALU.mult)\
                        .then_inc(normed, 1)

                for c in range(NC):
                    dve.wait_ge(x_in[c], 16)
                    norm(c, c)
                    if c:
                        scale(c - 1, c - 1)
                scale(NC - 1, NC - 1)

                dve.wait_ge(w_ready, R_SMALL + 1)
                dve.wait_ge(consts, 4)
                dve.tensor_scalar(u[:, :], bank(wbank(R_SMALL))[:, 0:H], 0.125, None, ALU.mult)
                dve.tensor_copy(wpad[:, 128 - H:128], bank(wbank(R_SMALL))[:, H:2 * H])
                dve.tensor_copy(kcol[:, :], bank(wbank(R_SMALL))[:, 2 * H:2 * H + 1]).then_inc(w_done, 1)
                for n in range(4):
                    dve.wait_ge(w_ready, R_WOT + n + 1)
                    dve.tensor_copy(woT[:, 4 * n:4 * n + 4, :], bank(wbank(R_WOT + n), DK, a=4)).then_inc(w_done, 1)
                for n in range(4):
                    dve.wait_ge(w_hi, n + 1)
                    dve.scalar_tensor_tensor(A_lo[:, 4 * n:4 * n + 4, :], bank(wbank(R_A + n), a=4), 0.125,
                                             A_hi[:, 4 * n:4 * n + 4, :].bitcast(F32), ALU.mult, ALU.subtract)\
                        .then_inc(w_done, 1)
                for n in range(4):
                    dve.wait_ge(w_hi, 4 + n + 1)
                    dve.tensor_tensor(VO[:, 4 * n:4 * n + 4, 1, :], bank(wbank(R_VO + n), a=4),
                                      VO[:, 4 * n:4 * n + 4, 0, :].bitcast(F32), ALU.subtract).then_inc(w_done, 1)
                dve.wait_ge(w_ready, R_CONST + 1)
                dve.tensor_copy(const_row[:, :], bank(wbank(R_CONST), S, D)).then_inc(w_done, 1)

                for c in range(NC):
                    dve.wait_ge(k_ready, c + 1)
                    dve.tensor_copy(kT[:, cols(c)], bank(4 + c, width=CB * S)).then_inc(k_copied, 1)
                for c in range(NC):
                    cs = slice(c * CB, (c + 1) * CB)
                    dve.wait_ge(s_ready, c + 1)
                    link(dve.tensor_tensor(chunk(pr, c), bank(4 + c, S, CB * S, a=CB),
                                           band[:, :].unsqueeze(1).to_broadcast([S, CB, S]), ALU.mult))
                    link(dve.tensor_reduce(rmax[:, cs], chunk(pr, c), AX.X, ALU.max))
                    dve.tensor_tensor(chunk(pr, c), chunk(pr, c),
                                      rmax[:, cs].unsqueeze(2).to_broadcast([S, CB, S]), ALU.subtract)\
                        .then_inc(s_shifted, 1)
                for c in range(NC):
                    cs = slice(c * CB, (c + 1) * CB)
                    dve.wait_ge(s_exp, c + 1)
                    link(dve.tensor_reduce(rsum[:, cs], chunk(pr, c), AX.X, ALU.add))
                    link(dve.reciprocal(rinv[:, cs], rsum[:, cs]))
                for c in range(NC):
                    dve.wait_ge(o_ready, c + 1)
                    for n in range(CB):
                        b = c * CB + n
                        last = dve.scalar_tensor_tensor(xt[:, b, :], bank(4 + c, S, a=CB)[:, n, :], rinv[:, b:b + 1],
                                                        xt[:, b, :], ALU.mult, ALU.add)
                    link(last)
                    norm(c, NC + c)
                    if c:
                        scale(c - 1, NC + c - 1)
                scale(NC - 1, 2 * NC - 1)
                for c in range(NC):
                    dve.tensor_tensor(chunk(xt, c), chunk(xt, c),
                                      const_row[:, :].unsqueeze(1).to_broadcast([S, CB, D]), ALU.add)\
                        .then_inc(x1_ready, 1)
                for c in range(NC):
                    dve.wait_ge(nT_hi, c + 1)
                    dve.tensor_tensor(n2lo[:, cols(c)], bank(c, width=CB * S), n2hi[:, cols(c)].bitcast(F32),
                                      ALU.subtract).then_inc(nT_lo, 1)
                dve.wait_ge(w_ready, R_C + 1)
                dve.tensor_scalar(c_all[:, :, 0:FT], bank(4, width=NB * FT, a=NB), kcol[:, 0:1], 0.125,
                                  ALU.add, ALU.mult)
                link(dve.tensor_scalar(c_all[:, :, FT:NT], bank(5, width=NB, a=NB), kcol[:, 0:1], 0.125,
                                       ALU.add, ALU.mult))

            @block.tensor
            def _(pe):
                pe.wait_ge(consts, 1)
                def w_free(r):
                    if r >= 4:
                        pe.wait_ge(w_done, r - 3)

                pe.wait_ge(wqk_in, 16 * 4)
                pe.wait_ge(bias_made, 1)
                pe.wait_ge(consts, 4)
                small = bank(wbank(R_SMALL))
                for h in range(H):
                    pe.matmul(small[:, h:h + 1], wK[:, h, :], bQ[:, h:h + 1], start=True, stop=True)
                    pe.matmul(small[:, H + h:H + h + 1], wQ[:, h, :], bK[:, h:h + 1], start=True, stop=True)
                pe.matmul(small[:, 2 * H:2 * H + 1], bbrep[:, :, :].rearrange("j q h -> j (q h)"), ones[:, 0:1],
                          start=True, stop=True).then_inc(w_ready, 1)
                for c in range(NC):
                    pe.wait_ge(normed, c + 1)
                    for n in range(CB):
                        last = pe.transpose(bank(c)[:, n * S:(n + 1) * S], nrm[:, c * CB + n, :], ident[0:S, 0:S])
                    last.then_inc(xT_ready, 1)
                pe.wait_ge(wv_in, 16 * 4)
                for n in range(4):
                    w_free(R_WOT + n)
                    for i in range(4):
                        h = 4 * n + i
                        last = pe.transpose(bank(wbank(R_WOT + n), DK, a=4)[:, i, :], wo[:, h * DK:(h + 1) * DK],
                                            ident[:, :])
                    last.then_inc(w_ready, 1)
                for n in range(4):
                    w_free(R_A + n)
                    for i in range(4):
                        h = 4 * n + i
                        last = pe.matmul(bank(wbank(R_A + n), a=4)[:, i, :], wQ[:, h, :], wK[:, h, :],
                                         start=True, stop=True)
                    last.then_inc(w_ready, 1)
                pe.wait_ge(w_done, R_WOT + 4)
                for n in range(4):
                    w_free(R_VO + n)
                    for i in range(4):
                        h = 4 * n + i
                        last = pe.matmul(bank(wbank(R_VO + n), a=4)[:, i, :], wV[:, h, :], woT[:, h, :],
                                         start=True, stop=True)
                    last.then_inc(w_ready, 1)
                w_free(R_CONST)
                pe.wait_ge(bias_made, 2)
                for h in range(H):
                    pe.matmul(bank(wbank(R_CONST), S, D), bVrep[:, h, :], woT[:, h, :], start=(h == 0), stop=False)
                pe.matmul(bank(wbank(R_CONST), S, D), ones[0:1, :], bo[:, :], start=False, stop=True)\
                    .then_inc(w_ready, 1)

                pe.wait_ge(self_in, 16 * 3)
                for c in range(NC):
                    pe.wait_ge(xT_copied, c + 1)
                    pe.matmul(bank(c, width=CB * S), wsq[:, :], xnT[:, cols(c)], start=True, stop=True)\
                        .then_inc(q_ready, 1)
                pe.wait_ge(w_done, R_CONST + 1)
                for c in range(NC):
                    pe.matmul(bank(4 + c, width=CB * S), wsk[:, :], xnT[:, cols(c)], start=True, stop=True)\
                        .then_inc(k_ready, 1)
                for c in range(NC):
                    pe.wait_ge(q_copied, c + 1)
                    for n in range(CB):
                        b = c * CB + n
                        last = pe.matmul(bank(c, S, a=CB)[:, n, :], xnT[:, b * S:(b + 1) * S], wsv[:, :],
                                         start=True, stop=True)
                    last.then_inc(v_ready, 1)
                for c in range(NC):
                    pe.wait_ge(k_copied, c + 1)
                    for n in range(CB):
                        b = c * CB + n
                        last = pe.matmul(bank(4 + c, S, CB * S, a=CB)[:, n, :], qT[:, b * S:(b + 1) * S],
                                         kT[:, b * S:(b + 1) * S], start=True, stop=True)
                    last.then_inc(s_ready, 1)
                for c in range(NC):
                    pe.wait_ge(v_copied, c + 1)
                    pe.wait_ge(s_exp, c + 1)
                    for n in range(CB):
                        last = pe.transpose(bank(c, S, CB * S, a=CB)[:, n, :], pr[:, c * CB + n, :],
                                            ident[0:S, 0:S])
                    last.then_inc(pT_ready, 1)
                for c in range(NC):
                    pe.wait_ge(pT_copied, c + 1)
                    pe.wait_ge(s_shifted, c + 1)
                    for n in range(CB):
                        b = c * CB + n
                        last = pe.matmul(bank(4 + c, S, a=CB)[:, n, :], prT[:, b, :], v[:, b, :],
                                         start=True, stop=True)
                    last.then_inc(o_ready, 1)
                for c in range(NC):
                    pe.wait_ge(normed, NC + c + 1)
                    for n in range(CB):
                        last = pe.transpose(bank(c)[:, n * S:(n + 1) * S], nrm[:, c * CB + n, :], ident[0:S, 0:S])
                    last.then_inc(nT_ready, 1)
                pe.wait_ge(nT_lo, NC)
                pe.wait_ge(w_done, 1)

                def c_rows(dst, first, n, step, offsets):
                    for part, xs in enumerate((n2hi, n2lo)):
                        xv = xs[:, :].bitcast(F32).rearrange("p (b q) -> p b q", b=NB)
                        for j in offsets:
                            xj = xv[:, :, first + j:first + j + step * (n - 1) + 1:step]
                            last = pe.matmul(dst, wpad[:, 128 - H - H * j:256 - H - H * j], xj,
                                             start=(part == 0 and j == 0), stop=(part == 1 and j == offsets[-1]))
                    return last

                c_rows(bank(4, width=NB * FT, a=NB), 0, FT, QR, range(QR))
                c_rows(bank(5, width=NB, a=NB), FT * QR, 1, 1, range(S - FT * QR)).then_inc(w_ready, 1)


def cross_attention(nc, ctx_in, mask, banks, ident, A_hi, A_lo, VO, u, c_all,
                    x1_dram, n2hi_dram, n2lo_dram, x2_dram):
    with ExitStack() as ctx:
        def sb(name, shape, dt=F32):
            return ctx.enter_context(nc.sbuf_tensor(name, shape, dt))

        def sem(name):
            return ctx.enter_context(nc.semaphore(name))

        def pair(name, shape, dt=F32):
            return [sb(f"{name}{i}", shape, dt) for i in range(2)]

        nat = sb("nat", [128, KT, D])
        ctx_hi, ctx_lo = pair("ctx_hi", [128, KT, D], F32R), pair("ctx_lo", [128, KT, D], F32R)
        ctxT_hi, ctxT_lo = pair("ctxT_hi", [128, SKP], F32R), pair("ctxT_lo", [128, SKP], F32R)
        qh, ql = pair("qh", [128, NT * 128], F32R), pair("ql", [128, NT * 128], F32R)
        qf = sb("qf", [128, 4, S])
        n2h, n2l = pair("n2h", [128, S], F32R), pair("n2l", [128, S], F32R)
        x1, x2 = pair("x1", [S, D]), pair("x2", [S, D])
        masks = [sb(f"mask{i}", [128, SK], U8) for i in range(MSLOTS)]
        mask_half = sb("mask_half", [HALF, SK], U8)
        bias = pair("bias", [128, SKP])
        probs = [sb(f"probs{i}", [128, SKP]) for i in range(PSLOTS)]
        probs_half = sb("probs_half", [HALF, SKP])
        pT_hi = [sb(f"pT_hi{i}", [128, 512], F32R) for i in range(TSLOTS)]
        pT_lo = [sb(f"pT_lo{i}", [128, 512], F32R) for i in range(TSLOTS)]
        oT_hi, oT_lo = sb("oT_hi", [128, S * H], F32R), sb("oT_lo", [128, S * H], F32R)
        c_cur = pair("c_cur", [128, NT])
        nmax = sb("nmax", [128, 2, PSLOTS + 1])
        rsum = sb("row_sum", [128, PSLOTS + 1])
        rinv = sb("row_inv", [128, PSLOTS + 1])

        zeroed = sem("zeroed")
        nat_in = sem("nat_in")
        passed_sp, passed_pool, passed_dve = sem("passed_sp"), sem("passed_pool"), sem("passed_dve")
        rows_in = [sem("rows_in0"), sem("rows_in1")]
        x1_in = [sem("x1_in0"), sem("x1_in1")]
        mask_in = [sem(f"mask_in{i}") for i in range(MSLOTS)]
        mask_half_in = sem("mask_half_in")
        c_here = sem("c_here")
        ctx_split = sem("ctx_split")
        ctx_hi_made = sem("ctx_hi_made")
        bias_ready = sem("bias_ready")
        scores_ready, scores_taken = sem("scores_ready"), sem("scores_taken")
        exp_done, recip_done, probs_ready = sem("exp_done"), sem("recip_done"), sem("probs_ready")
        turned, turned_hi, turned_lo = sem("turned"), sem("turned_hi"), sem("turned_lo")
        values_done = sem("values_done")
        out_hi, out_lo = sem("out_hi"), sem("out_lo")
        prep_ready, prep_hi, prep_read = sem("prep_ready"), sem("prep_hi"), sem("prep_read")
        q_split = sem("q_split")
        qf_used = sem("qf_used")
        x2_begun = sem("x2_begun")
        proj_ready, x2_ready, x2_stored = sem("proj_ready"), sem("x2_ready"), sem("x2_stored")

        S_BANK, T_BANK, O_BANK = 0, 4, 6

        def out_bank(g):
            return O_BANK + g % 2

        def misc_bank(kind, r):
            return O_BANK + 1 - ROUNDS[kind, r][0] % 2

        def tslot(b_odd, j):
            return (NSTEP * b_odd + j) % TSLOTS

        def slot(t):
            return t % PSLOTS if t < FT else PSLOTS

        def prob(t):
            return probs[t % PSLOTS] if t < FT else probs_half

        def known(b):
            return isinstance(b, int)

        def here(b, db):
            return not known(b) or 0 <= b + db < NB

        def wait(engine, sem, b, per, plus):
            if not known(b) or b * per + plus > 0:
                engine.wait_ge(sem, at(b, per, plus))

        def periods(engine, emit):
            emit(-1, 1)
            emit(0, 0)
            with engine.Fori(1, NB - 2, 2) as b:
                emit(b, 1)
                emit(b + 1, 0)
            emit(NB - 1, 1)
            emit(NB, 0)

        with nc.Block() as block:
            @block.sync
            def _(sp):
                sp.wait_ge(zeroed, 2 * 3 + 1)

                def load_rows(b, odd):
                    wait_apart(sp, ctx_split, b, 3, 0, passed_sp)
                    wait_apart(sp, prep_ready, b, PREP, 3 - PREP, passed_sp)
                    c = ctx_in[b] if known(b) else ctx_in[bass.ds(b, 1)].rearrange("a k d -> (a k) d")
                    sp.dma_start(nat[:, 0:KT - 1, :], c[0:(KT - 1) * 128, :].rearrange("(t p) d -> p t d", p=128))\
                        .then_inc(nat_in, 16)
                    sp.dma_start(nat[SHIFT:SHIFT + LASTK, KT - 1, :], c[(KT - 1) * 128:SK, :]).then_inc(nat_in, 16)
                    for t, w in ((n2h, n2hi_dram), (n2l, n2lo_dram)):
                        wait_apart(sp, prep_ready, b, PREP, -PREP, passed_sp)
                        w_b = w[b] if known(b) else w[bass.ds(b, 1)].rearrange("a k d -> (a k) d")
                        sp.dma_start(t[odd][:, :].bitcast(F32), w_b).then_inc(rows_in[odd], 16)

                def load_x1(b, odd):
                    x_b = x1_dram[b] if known(b) else x1_dram[bass.ds(b, 1)].rearrange("a k d -> (a k) d")
                    sp.dma_start(x1[odd][:, :], x_b).then_inc(x1_in[odd], 16)

                def load_mask(b, t):
                    q0, nq = t * QR, rows_of(t) // H
                    if known(b):
                        src = mask[b, q0:q0 + nq, :]
                    else:
                        src = mask[bass.ds(b, 1), q0:q0 + nq, :].rearrange("a q k -> (a q) k")
                    dst = masks[t % MSLOTS] if t < FT else mask_half
                    if t < FT:
                        before = t - MSLOTS + 1 if t >= MSLOTS else t - MSLOTS - 1 + 1
                        wait_apart(sp, bias_ready, b, NT, before, passed_sp)
                    else:
                        wait_apart(sp, bias_ready, b, NT, 0, passed_sp)
                    sp.dma_start(dst[:, :], src.unsqueeze(1).to_broadcast([nq, H, SK]))\
                        .then_inc(mask_in[t % MSLOTS] if t < FT else mask_half_in, 16)

                def emit(b, odd):
                    if here(b, 1):
                        load_rows(b + 1, 1 - odd)
                    if known(b) and b < 0:
                        load_x1(0, 0)
                    for t in range(NT):
                        if here(b, 0):
                            load_mask(b, t)
                        if t == 9 and here(b, -1):
                            wait_apart(sp, x2_ready, b, 1, 0, passed_sp)
                            dst = x2_dram[bass.ds((b - 1) * S, S), :] if not known(b) else \
                                x2_dram[(b - 1) * S:b * S, :]
                            sp.dma_start(dst, x2[1 - odd][:, :]).then_inc(x2_stored, 16)
                    if here(b, 0) and here(b, 1):
                        wait_apart(sp, x2_stored, b, 16, 0, passed_sp)
                        load_x1(b + 1, 1 - odd)

                periods(sp, emit)
                sp.wait_ge(x2_stored, 16 * NB)

            @block.gpsimd
            def _(pool):
                pool.memset(nat[:, KT - 1, :], 0.0).then_inc(zeroed, 1)
                for i in range(2):
                    pool.memset(bias[i][:, SK:SKP], PAD).then_inc(zeroed, 1)
                    for t in (qh, ql):
                        pool.memset(t[i][:, S * H:NT * 128].bitcast(F32), 0.0).then_inc(zeroed, 1)

                order = pool_order()

                def emit(b, odd):
                    def make_bias(db, t):
                        i = odd if db == 0 else 1 - odd
                        n = rows_of(t)
                        if t == 0:
                            b_abs = b + db
                            wait(pool, bias_ready, b_abs, NT, -NT)
                            src = c_all[:, b_abs, :] if known(b_abs) else \
                                c_all[:, bass.ds(b_abs, 1), :].rearrange("p a t -> p (a t)")
                            pool.tensor_copy(c_cur[i][:, :], src).then_inc(c_here, 1)
                            wait(pool, c_here, b_abs, 1, 1)
                        if t < FT:
                            wait(pool, mask_in[t % MSLOTS], b + db, 16 * (FT // MSLOTS), 16 * (t // MSLOTS + 1))
                        else:
                            wait(pool, mask_half_in, b + db, 16, 16)
                        wait_apart(pool, scores_taken, b + db, 2 * NT, 2 * (t - 1), passed_pool)
                        src = masks[t % MSLOTS] if t < FT else mask_half
                        pool.tensor_scalar(bias[(t + i) % 2][0:n, 0:SK], src[:, :], MASKED, c_cur[i][0:n, t:t + 1],
                                           ALU.mult, ALU.add).then_inc(bias_ready, 1)

                    for _, kind, db, j in order:
                        if not here(b, db):
                            continue
                        if kind == "bias":
                            make_bias(db, j)
                        elif kind == "norm":
                            wait_apart(pool, recip_done, b + db, NT, j + 1, passed_pool)
                            n, s = rows_of(j), slot(j)
                            pool.tensor_scalar(prob(j)[0:n, :], prob(j)[0:n, :], rinv[0:n, s:s + 1], 1.0,
                                               ALU.mult, ALU.mult).then_inc(probs_ready, 1)
                        elif kind == "split":
                            i = 1 - odd
                            part = slice(4 * j, 4 * j + 4)
                            if j == 0:
                                wait(pool, values_done, b + db, NSTEP, -NSTEP)
                                wait_apart(pool, nat_in, b + db, 32, 32, passed_pool)
                            pool.tensor_scalar(ctx_hi[i][:, part, :], nat[:, part, :], 1.0, 1.0, ALU.mult, ALU.mult)\
                                .then_inc(ctx_hi_made, 1)
                            wait(pool, ctx_hi_made, b + db, 3, j + 1)
                            pool.tensor_tensor(ctx_lo[i][:, part, :], nat[:, part, :],
                                               ctx_hi[i][:, part, :].bitcast(F32), ALU.subtract)\
                                .then_inc(ctx_split, 1)
                        elif kind == "prep":
                            i, n = 1 - odd, j - 3
                            wait(pool, prep_hi, b + db, PREP, j + 1)
                            dst = ql[i][:, 0:S * H].rearrange("p (q h) -> p h q", h=H)[:, 4 * n:4 * n + 4, :]
                            hi = qh[i][:, 0:S * H].rearrange("p (q h) -> p h q", h=H)[:, 4 * n:4 * n + 4, :]
                            pool.tensor_tensor(dst, qf[:, :, :], hi.bitcast(F32), ALU.subtract)\
                                .then_inc(q_split, 1)

                def start():
                    pool.wait_ge(zeroed, 2 * 3 + 1)

                start()
                periods(pool, emit)

            @block.scalar
            def _(act):
                order = act_order()

                def emit(b, odd):
                    for _, kind, db, j in order:
                        if not here(b, db):
                            continue
                        i = odd if db == 0 else 1 - odd
                        if kind == "exp":
                            n, s = rows_of(j), slot(j)
                            wait(act, scores_taken, b + db, 2 * NT, 2 * j + 2)
                            act.activation(prob(j)[0:n, :], prob(j)[0:n, :], ACT.Exp,
                                           bias=nmax[0:n, 1, s:s + 1], scale=-1.0,
                                           accum_out=rsum[0:n, s:s + 1]).then_inc(exp_done, 1)
                        elif kind == "step":
                            g, _ = STEPS[j]
                            w = WIDTH[g] * KPB[g]
                            wait(act, turned, b + db, NSTEP, j + 1)
                            wait(act, values_done, b + db, NSTEP, j + 1 - TSLOTS)
                            act.copy(pT_hi[tslot(i, j)][:, 0:w], banks[:, T_BANK + j % 2, 0:w]).then_inc(turned_hi, 1)
                        elif kind == "out":
                            wait(act, values_done, b + db, NSTEP, steps_to(j))
                            wait(act, proj_ready, b + db, 1, 0)
                            cs = slice(256 * j, 256 * j + WIDTH[j])
                            act.copy(oT_hi[:, cs], banks[:, out_bank(j), 0:WIDTH[j]]).then_inc(out_hi, 1)
                        elif kind == "prep":
                            if j < 3:
                                wait(act, prep_ready, b + db, PREP, j + 1)
                                w = min(512, SKP - 512 * j)
                                src = banks[:, misc_bank(kind, j), 0:512]
                                if j == 2:
                                    act.copy(ctxT_hi[i][:, 1024:1408], src[:, 0:384])
                                    act.copy(ctxT_hi[i][:, 1408:SKP], src[:, 384 + SHIFT:512]).then_inc(prep_hi, 1)
                                else:
                                    act.copy(ctxT_hi[i][:, 512 * j:512 * j + w], src[:, 0:w]).then_inc(prep_hi, 1)
                            else:
                                wait(act, prep_read, b + db, PREP, j + 1)
                                n = j - 3
                                dst = qh[i][:, 0:S * H].rearrange("p (q h) -> p h q", h=H)[:, 4 * n:4 * n + 4, :]
                                act.copy(dst, qf[:, :, :]).then_inc(prep_hi, 1)

                periods(act, emit)

            @block.vector
            def _(dve):
                order = dve_order()

                def emit(b, odd):
                    for _, kind, db, j in order:
                        if not here(b, db):
                            continue
                        i = odd if db == 0 else 1 - odd
                        if kind == "score":
                            t, half = j // 2, j % 2
                            n, s = rows_of(t), slot(t)
                            if half == 0:
                                wait(dve, bias_ready, b + db, NT, t + 1)
                                if t >= FT:
                                    wait(dve, turned, b + db, NSTEP, 0)
                                elif t >= PSLOTS:
                                    wait(dve, turned, b + db, NSTEP, steps_to(group_of(t - PSLOTS)))
                                else:
                                    wait(dve, turned, b + db, NSTEP, steps_to(group_of(t + PSLOTS)) - NSTEP)
                            else:
                                wait(dve, scores_taken, b + db, 2 * NT, j)
                            wait_apart(dve, scores_ready, b + db, 2 * NT, j + 1, passed_dve)
                            cs = slice(half * 2 * CW, (half + 1) * 2 * CW)
                            src = banks[0:n, S_BANK + 2 * half:S_BANK + 2 * half + 2, 0:CW]
                            first = -PAD if half == 0 else nmax[0:n, 0, s:s + 1]
                            dve.tensor_tensor_reduce(
                                prob(t)[0:n, cs].rearrange("p (a k) -> p a k", a=2), src,
                                bias[(t + i) % 2][0:n, cs].rearrange("p (a k) -> p a k", a=2), -1.0, first,
                                ALU.add, ALU.min, nmax[0:n, half, s:s + 1]).then_inc(scores_taken, 1)
                        elif kind == "recip":
                            n, s = rows_of(j), slot(j)
                            wait(dve, exp_done, b + db, NT, j + 1)
                            dve.reciprocal(rinv[0:n, s:s + 1], rsum[0:n, s:s + 1]).then_inc(recip_done, 1)
                        elif kind == "step":
                            g, _ = STEPS[j]
                            w = WIDTH[g] * KPB[g]
                            wait(dve, turned_hi, b + db, NSTEP, j + 1)
                            dve.tensor_tensor(pT_lo[tslot(i, j)][:, 0:w], banks[:, T_BANK + j % 2, 0:w],
                                              pT_hi[tslot(i, j)][:, 0:w].bitcast(F32), ALU.subtract)\
                                .then_inc(turned_lo, 1)
                        elif kind == "out":
                            wait(dve, out_hi, b + db, NG, j + 1)
                            cs = slice(256 * j, 256 * j + WIDTH[j])
                            dve.tensor_tensor(oT_lo[:, cs], banks[:, out_bank(j), 0:WIDTH[j]], oT_hi[:, cs].bitcast(F32),
                                              ALU.subtract).then_inc(out_lo, 1)
                        elif kind == "prep":
                            src = banks[:, misc_bank(kind, j), 0:512]
                            if j < 3:
                                wait(dve, prep_hi, b + db, PREP, j + 1)
                                w = min(512, SKP - 512 * j)
                                if j == 2:
                                    dve.tensor_tensor(ctxT_lo[i][:, 1024:1408], src[:, 0:384],
                                                      ctxT_hi[i][:, 1024:1408].bitcast(F32), ALU.subtract)
                                    dve.tensor_tensor(ctxT_lo[i][:, 1408:SKP], src[:, 384 + SHIFT:512],
                                                      ctxT_hi[i][:, 1408:SKP].bitcast(F32), ALU.subtract)\
                                        .then_inc(prep_read, 1)
                                else:
                                    dve.tensor_tensor(ctxT_lo[i][:, 512 * j:512 * j + w], src[:, 0:w],
                                                      ctxT_hi[i][:, 512 * j:512 * j + w].bitcast(F32), ALU.subtract)\
                                        .then_inc(prep_read, 1)
                            else:
                                wait(dve, prep_ready, b + db, PREP, j + 1)
                                n = j - 3
                                wait(dve, q_split, b + db, 4, n)
                                dve.tensor_tensor(qf[:, :, :], src[:, 0:4 * S].rearrange("p (h q) -> p h q", h=4),
                                                  u[:, 4 * n:4 * n + 4].unsqueeze(2).to_broadcast([128, 4, S]),
                                                  ALU.add).then_inc(prep_read, 1)
                        elif kind == "project":
                            wait(dve, proj_ready, b + db, 1, 1)
                            wait(dve, x1_in[i], b + db, 8, 8 if i else 16)
                            out_main, out_rest = (banks[0:S, misc_bank(kind, 0), n * D:(n + 1) * D] for n in range(2))
                            dve.tensor_tensor(x2[i][:, :], out_main, x1[i][:, :], ALU.add).then_inc(x2_begun, 1)
                            wait(dve, x2_begun, b + db, 1, 1)
                            dve.tensor_tensor(x2[i][:, :], out_rest, x2[i][:, :], ALU.add).then_inc(x2_ready, 1)

                periods(dve, emit)

            @block.tensor
            def _(pe):
                pe.wait_ge(zeroed, 2 * 3 + 1)

                def score(b, i, n):
                    t, half = n // 2, n % 2
                    rows = slice(t * 128, (t + 1) * 128)
                    if n == 0:
                        wait(pe, q_split, b, 4, 4)
                        wait(pe, prep_read, b, PREP, PREP)
                    wait(pe, scores_taken, b, 2 * NT, n - 1)
                    for qpart, kparts in ((qh[i], (ctxT_hi[i], ctxT_lo[i])), (ql[i], (ctxT_hi[i],))):
                        for kpart in kparts:
                            first = qpart is qh[i] and kpart is ctxT_hi[i]
                            for c in (2 * half, 2 * half + 1):
                                last = pe.matmul(banks[:, S_BANK + c, 0:CW], qpart[:, rows],
                                                 kpart[:, c * CW:(c + 1) * CW], start=first, stop=qpart is ql[i])
                    last.then_inc(scores_ready, 1)

                def turn(b, j):
                    g, k0 = STEPS[j]
                    if k0 == 0:
                        wait(pe, probs_ready, b, NT, tiles_of(g)[-1] + 1)
                    wait(pe, turned_lo, b, NSTEP, j - 1)
                    for kk in range(KPB[g]):
                        k = k0 + kk
                        c0 = k * 128 if k < KT - 1 else SKP - 128
                        for n, t in enumerate(tiles_of(g)):
                            r = rows_of(t)
                            at_col = kk * WIDTH[g] + n * 128
                            last = pe.transpose(banks[:, T_BANK + j % 2, at_col:at_col + r],
                                                prob(t)[0:r, c0:c0 + 128], ident[0:r, 0:r])
                    last.then_inc(turned, 1)

                def values(b, i, j):
                    g, k0 = STEPS[j]
                    w = WIDTH[g]
                    wait(pe, turned_lo, b, NSTEP, j + 1)
                    if k0 == 0:
                        wait(pe, out_lo, b, NG, g - 1)
                        kind, db, r = GROUPS[g]
                        if kind == "project":
                            wait(pe, x2_ready, b + db, 1, 1)
                        elif known(b):
                            pe.wait_ge(prep_read, min(PREP * (b + db) + r + 1, PREP * NB))
                        else:
                            wait(pe, prep_read, b + db, PREP, r + 1)
                        if g == 0:
                            wait(pe, ctx_split, b, 3, 3)
                    for kk in range(KPB[g]):
                        k = k0 + kk
                        cs = slice(kk * w, (kk + 1) * w)
                        for stationary, moving in ((ctx_hi[i], pT_hi), (ctx_hi[i], pT_lo), (ctx_lo[i], pT_hi)):
                            last = pe.matmul(banks[:, out_bank(g), 0:w], stationary[:, k, :], moving[tslot(i, j)][:, cs],
                                             start=(k == 0 and stationary is ctx_hi[i] and moving is pT_hi),
                                             stop=(k == KT - 1 and stationary is ctx_lo[i]))
                    last.then_inc(values_done, 1)

                def prep(b, i, r):
                    wait(pe, prep_read, b, PREP, r)
                    wait(pe, x2_ready, b, 1, -1)
                    g, dd = ROUNDS["prep", r]
                    wait(pe, out_lo, b - 1 + dd, NG, g)
                    bank = misc_bank("prep", r)
                    if r < 3:
                        if r == 0:
                            wait(pe, nat_in, b, 32, 32)
                        for n in range(4):
                            last = pe.transpose(banks[:, bank, n * 128:(n + 1) * 128], nat[:, 4 * r + n, :], ident[:, :])
                    else:
                        if r == 3:
                            wait(pe, rows_in[i], b, 16, 16 if i else 32)
                        for n in range(4):
                            h = 4 * (r - 3) + n
                            dst = banks[:, bank, n * S:(n + 1) * S]
                            pe.matmul(dst, A_hi[:, h, :], n2h[i][:, :], start=True, stop=False)
                            pe.matmul(dst, A_hi[:, h, :], n2l[i][:, :], start=False, stop=False)
                            last = pe.matmul(dst, A_lo[:, h, :], n2h[i][:, :], start=False, stop=True)
                    last.then_inc(prep_ready, 1)

                def project(b):
                    wait(pe, out_lo, b, NG, NG)
                    if known(b):
                        pe.wait_ge(prep_read, min(PREP * (b + 2), PREP * NB))
                    else:
                        wait(pe, prep_read, b, PREP, 2 * PREP)
                    both, main = (banks[0:S, misc_bank("project", 0), 0:w] for w in (2 * D, D))
                    for h in range(H):
                        last_head = h == H - 1
                        if not last_head:
                            pe.matmul(both, oT_hi[:, h:S * H:H], VO[:, h, :, :].rearrange("p a d -> p (a d)"),
                                      start=(h == 0), stop=False)
                        pe.matmul(main, oT_lo[:, h:S * H:H], VO[:, h, 0, :], start=False, stop=False)
                        if last_head:
                            pe.matmul(both, oT_hi[:, h:S * H:H], VO[:, h, :, :].rearrange("p a d -> p (a d)"),
                                      start=False, stop=True).then_inc(proj_ready, 1)

                def emit(b, odd):
                    for _, kind, db, j in ORDER:
                        if kind == "step":
                            jj, dd = lagged(j, db)
                            if here(b, dd):
                                values(b + dd, odd if dd % 2 == 0 else 1 - odd, jj)
                            if here(b, db):
                                turn(b + db, j)
                        elif not here(b, db):
                            continue
                        elif kind == "score":
                            score(b + db, odd, j)
                        elif kind == "prep":
                            prep(b + db, 1 - odd, j)
                        elif kind == "project":
                            project(b + db)

                periods(pe, emit)


TT = (NTOK + 127) // 128
TPAD = TT * 128
TG = [slice(4 * g, min(4 * g + 4, TT)) for g in range((TT + 3) // 4)]
NTG = len(TG)
LASTROWS = NTOK - (TT - 1) * 128
CT = 400
UNITS = [(m, c) for c in range(NTOK // CT) for m in range(HID // 128)]
NU = len(UNITS)


def experts(nc, Wg, W1, b1, W11, b11, W2, b2, Ws1, bs1, Ws11, bs11, Ws2, bs2,
            banks, ident, x2_dram, out):
    with ExitStack() as ctx:
        def sb(name, shape, dt=F32):
            return ctx.enter_context(nc.sbuf_tensor(name, shape, dt))

        def sem(name):
            return ctx.enter_context(nc.semaphore(name))

        def pair(name, shape, dt=F32):
            return [sb(f"{name}{i}", shape, dt) for i in range(2)]

        y = sb("y", [128, TT, D])
        cen3, nrm3 = sb("cen3", [128, TT, D]), sb("nrm3", [128, TT, D])
        sq3 = sb("sq3", [128, 4, D])
        st3 = sb("st3", [128, 5, TT])
        t_hi, t_lo = sb("t_hi", [128, TPAD], F32R), sb("t_lo", [128, TPAD], F32R)
        wg, wg_hi, wg_lo = sb("wg", [128, NE]), sb("wg_hi", [128, NE], F32R), sb("wg_lo", [128, NE], F32R)
        b_rows, b_cols = sb("b_rows", [2 * NX, 2, 128]), sb("b_cols", [128, 2, 2 * NX])
        b2_rows = sb("b2_rows", [NE + 1, D])
        logits = sb("logits", [128, TT, NE])
        order16 = sb("order16", [128, NE])
        rank = sb("rank", [128, TT, NE])
        top = sb("top", [128, 6, TT])
        pick = [sb(f"pick{i}", [128, TT, NE]) for i in range(2)]
        gates = sb("gates", [128, TT, NX])
        gatesT = sb("gatesT", [NX, TPAD])
        gate_rows = pair("gate_rows", [128, NTOK])
        yT = sb("yT", [128, TPAD])
        w_raw = pair("w_raw", [128, 3, HID])
        w_hi, w_lo = pair("w_hi", [128, 3, HID], F32R), pair("w_lo", [128, 3, HID], F32R)
        act_out, hid, gated = pair("act_out", [128, CT]), pair("hid", [128, CT]), sb("gated", [128, 4, CT])
        h_hi, h_lo = pair("h_hi", [128, 2, NTOK], F32R), pair("h_lo", [128, 2, NTOK], F32R)
        gates_dram = nc.dram_tensor("gates_dram", (NX, NTOK), F32, kind="Internal").ap()

        e_x_in = [sem(f"e_x_in{g}") for g in range(NTG)]
        e_small_in, w_in = sem("e_small_in"), [sem("w_in0"), sem("w_in1")]
        passed_act = sem("passed_act")
        e_consts = sem("e_consts")
        e_chain, e_pool_chain = sem("e_chain"), sem("e_pool_chain")
        e_var, e_std, e_normed = sem("e_var"), sem("e_std"), sem("e_normed")
        tT_ready, tT_hi, tT_lo = sem("tT_ready"), sem("tT_hi"), sem("tT_lo")
        wg_split = sem("wg_split")
        b_ready, b_copied = sem("b_ready"), sem("b_copied")
        l_ready = sem("l_ready")
        g_diff, g_exp, g_done = sem("g_diff"), sem("g_exp"), sem("g_done")
        gT_ready, gT_copied = sem("gT_ready"), sem("gT_copied")
        gates_stored, gates_in = sem("gates_stored"), [sem("gates_in0"), sem("gates_in1")]
        gated_done = sem("gated_done")
        up_hi, up_split = sem("up_hi"), sem("up_split")
        down_hi, down_split = sem("down_hi"), sem("down_split")
        ab_ready, silu_done, hid_done = sem("ab_ready"), sem("silu_done"), sem("hid_done")
        hhi_done, hlo_done = sem("hhi_done"), sem("hlo_done")
        out_done, out_copied = sem("out_done"), sem("out_copied")
        y_turned, y_added = sem("y_turned"), sem("y_added")
        e_stored = sem("e_stored")

        def known(e):
            return isinstance(e, int)

        def wait(engine, sem, e, per, plus):
            if not known(e) or e * per + plus > 0:
                engine.wait_ge(sem, at(e, per, plus))

        def bank(n, rows=128, width=512, a=None):
            p = banks[0:rows, n, 0:width]
            return p if a is None else p.rearrange("p (a n) -> p a n", a=a)

        def tcols(g):
            return slice(TG[g].start * 128, TG[g].stop * 128)

        def ntiles(g):
            return TG[g].stop - TG[g].start

        def turns(engine, emit):
            emit(0, 0)
            with engine.Fori(1, NX - 2, 2) as e:
                emit(e, 1)
                emit(e + 1, 0)
            emit(NX - 1, 1)
            emit(NX, 0)

        def behind(e, odd, n):
            if n >= 2:
                return None if known(e) and e == NX else (e, odd, n - 2)
            return None if known(e) and e == 0 else (e - 1, 1 - odd, n - 2 + NU)

        with nc.Block() as block:
            @block.sync
            def _(sp):
                for g in range(NTG - 1):
                    sp.dma_start(y[:, TG[g], :], x2_dram[tcols(g), :].rearrange("(t p) d -> p t d", p=128))\
                        .then_inc(e_x_in[g], 16)
                sp.dma_start(y[0:LASTROWS, TT - 1, :], x2_dram[(TT - 1) * 128:NTOK, :])\
                    .then_inc(e_x_in[NTG - 1], 16)

                def load(e, odd, a, b, c):
                    wait(sp, down_split, e, 1, -1)
                    for n, w in enumerate((a, b)):
                        sp.dma_start(w_raw[odd][:, n, :], w).then_inc(w_in[odd], 16)
                    sp.dma_start(w_raw[odd][:, 2, :].rearrange("p (m d) -> p m d", m=2),
                                 c.rearrange("(m p) d -> p m d", p=128)).then_inc(w_in[odd], 16)

                def load_gates(e, odd, row):
                    wait(sp, gated_done, e, NU, -NU)
                    sp.dma_start(gate_rows[odd][:, :], row.to_broadcast([128, NTOK])).then_inc(gates_in[odd], 16)

                load(0, 0, W1[0], W11[0], W2[0])
                load(1, 1, W1[1], W11[1], W2[1])
                sp.wait_ge(gates_stored, 16)
                for e in range(2):
                    load_gates(e, e, gates_dram[e:e + 1, :])
                with sp.Fori(2, NE - 1, 2) as e:
                    for odd in range(2):
                        one = bass.ds(e + odd, 1)
                        load(e + odd, odd, *(w[one].rearrange("a k d -> (a k) d") for w in (W1, W11, W2)))
                        load_gates(e + odd, odd, gates_dram[one, :])
                for n in range(2):
                    cs = slice(n * HID, (n + 1) * HID)
                    load(NE + n, n, Ws1[:, cs], Ws11[:, cs], Ws2[cs, :])
                    load_gates(NE + n, n, gates_dram[NE + n:NE + n + 1, :])
                for g in range(NTG):
                    sp.wait_ge(y_added, g + 1)
                    if g < NTG - 1:
                        sp.dma_start(out[tcols(g), :].rearrange("(t p) d -> p t d", p=128), y[:, TG[g], :])\
                            .then_inc(e_stored, 16)
                    else:
                        sp.dma_start(out[(TT - 1) * 128:NTOK, :], y[0:LASTROWS, TT - 1, :]).then_inc(e_stored, 16)
                sp.wait_ge(e_stored, 16 * NTG)

            @block.gpsimd
            def _(pool):
                for n in range(NE):
                    pool.memset(order16[:, n:n + 1], float(NE - n)).then_inc(e_consts, 1)
                pool.memset(gates[:, :, NE:NX], 1.0).then_inc(e_consts, 1)

                def emit(e, odd):
                    if known(e) and e == NX:
                        return
                    wait(pool, gates_in[odd], e, 8, 8 + (8 if odd == 0 else 0))
                    for n, (m, c) in enumerate(UNITS):
                        wait(pool, hid_done, e, NU, n + 1)
                        wait(pool, hlo_done, e, NU, n - 3)
                        pool.tensor_tensor(gated[:, n % 4, :], hid[n % 2][:, :],
                                           gate_rows[odd][:, c * CT:(c + 1) * CT], ALU.mult).then_inc(gated_done, 1)

                turns(pool, emit)

            @block.scalar
            def _(act):
                act.dma_start(wg[:, :], Wg).then_inc(e_small_in, 16)
                for n, (routed, shared) in enumerate(((b1, bs1), (b11, bs11))):
                    act.dma_start(b_rows[0:2 * NE, n, :], routed.rearrange("e (m p) -> (e m) p", p=128))\
                        .then_inc(e_small_in, 16)
                    act.dma_start(b_rows[2 * NE:2 * NX, n, :], shared.rearrange("(m p) -> m p", p=128))\
                        .then_inc(e_small_in, 16)
                act.dma_start(b2_rows[0:NE, :], b2).then_inc(e_small_in, 16)
                act.dma_start(b2_rows[NE:NE + 1, :], bs2.rearrange("(a d) -> a d", a=1)).then_inc(e_small_in, 16)
                def std(g):
                    act.wait_ge(e_var, g + 1)
                    act.activation(st3[:, 3, TG[g]], st3[:, 2, TG[g]], ACT.Sqrt).then_inc(e_std, 1)


                def split_up(e, odd):
                    wait(act, w_in[odd], e, 24, 24 + (24 if odd == 0 else 0))
                    wait(act, ab_ready, e, NU, -NU)
                    act.copy(w_hi[odd][:, 0:2, :], w_raw[odd][:, 0:2, :]).then_inc(up_hi, 1)

                def split_down(e, odd):
                    wait(act, out_done, e, NTG, -NTG)
                    act.copy(w_hi[odd][:, 2, :], w_raw[odd][:, 2, :]).then_inc(down_hi, 1)

                std(0)
                for g in range(NTG):
                    if g + 1 < NTG:
                        std(g + 1)
                    act.wait_ge(tT_ready, g + 1)
                    act.copy(t_hi[:, tcols(g)], bank(g, width=128 * ntiles(g))).then_inc(tT_hi, 1)
                split_up(0, 0)
                act.wait_ge(b_ready, 1)
                act.copy(b_cols[:, :, :], bank(7, width=4 * NX, a=2)).then_inc(b_copied, 1)
                act.wait_ge(g_diff, 1)
                act.activation(top[:, 3, :], top[:, 2, :], ACT.Exp).then_inc(g_exp, 1)
                for g in range(NTG):
                    act.wait_ge(gT_ready, g + 1)
                    act.copy(gatesT[:, tcols(g)], bank(g, NX, 128 * ntiles(g))).then_inc(gT_copied, 1)
                act.wait_ge(gT_copied, NTG)
                act.dma_start(gates_dram[:, :], gatesT[:, 0:NTOK]).then_inc(gates_stored, 16)

                def emit(e, odd):
                    for n in range(NU):
                        if behind(e, odd, n):
                            be, bodd, bn = behind(e, odd, n)
                            m, c = UNITS[bn]
                            wait(act, gated_done, be, NU, bn + 1)
                            if bn == 0:
                                wait(act, out_done, be, NTG, -NTG)
                            act.copy(h_hi[bodd][:, m, c * CT:(c + 1) * CT], gated[:, bn % 4, :]).then_inc(hhi_done, 1)
                        if known(e) and e == NX:
                            continue
                        m, c = UNITS[n]
                        wait(act, hid_done, e, NU, n - 1)
                        wait_apart(act, ab_ready, e, NU, n + 1, passed_act)
                        j = 2 * e + m
                        bias = b_cols[:, 0, j:j + 1] if known(e) else b_cols[:, 0, bass.ds(j, 1)]
                        act.activation(act_out[n % 2][:, :], bank(2 * (n % 2), width=CT), ACT.Silu,
                                       bias=bias).then_inc(silu_done, 1)
                        if n == 2:
                            split_down(e, odd)
                        if n == 5 and not (known(e) and e + 1 >= NX):
                            split_up(e + 1, 1 - odd)

                turns(act, emit)
                for g in range(0, NTG, 2):
                    act.wait_ge(out_done, (NX - 1) * NTG + g + 1)
                    act.copy(yT[:, g * CT:(g + 1) * CT], bank(4 + g, width=CT)).then_inc(out_copied, 1)

            @block.vector
            def _(dve):
                link = Chain(dve, e_chain)
                dve.memset(y[LASTROWS:128, TT - 1, :], 0.0)

                def norm(g):
                    ts, n = TG[g], ntiles(g)
                    wide = [128, n, D]
                    dve.wait_ge(e_x_in[g], 16)
                    link(dve.tensor_reduce(st3[:, 0, ts], y[:, ts, :], AX.X, ALU.add))
                    link(dve.tensor_scalar(st3[:, 1, ts], st3[:, 0, ts], 1.0 / D, None, ALU.mult))
                    link(dve.tensor_tensor(cen3[:, ts, :], y[:, ts, :],
                                           st3[:, 1, ts].unsqueeze(2).to_broadcast(wide), ALU.subtract))
                    link(dve.tensor_tensor(sq3[:, 0:n, :], cen3[:, ts, :], cen3[:, ts, :], ALU.mult))
                    link(dve.tensor_reduce(st3[:, 0, ts], sq3[:, 0:n, :], AX.X, ALU.add))
                    dve.tensor_scalar(st3[:, 2, ts], st3[:, 0, ts], 1.0 / D, EPS, ALU.mult, ALU.add).then_inc(e_var, 1)

                def scale(g):
                    ts = TG[g]
                    dve.wait_ge(e_std, g + 1)
                    link(dve.reciprocal(st3[:, 4, ts], st3[:, 3, ts]))
                    dve.tensor_tensor(nrm3[:, ts, :], cen3[:, ts, :],
                                      st3[:, 4, ts].unsqueeze(2).to_broadcast([128, ntiles(g), D]), ALU.mult)\
                        .then_inc(e_normed, 1)

                for g in range(NTG):
                    norm(g)
                    if g:
                        scale(g - 1)
                scale(NTG - 1)
                dve.wait_ge(e_small_in, 16 * 7)
                link(dve.tensor_copy(wg_hi[:, :], wg[:, :]))
                dve.tensor_tensor(wg_lo[:, :], wg[:, :], wg_hi[:, :].bitcast(F32), ALU.subtract).then_inc(wg_split, 1)
                for g in range(NTG):
                    dve.wait_ge(tT_hi, g + 1)
                    dve.tensor_tensor(t_lo[:, tcols(g)], bank(g, width=128 * ntiles(g)), t_hi[:, tcols(g)].bitcast(F32),
                                      ALU.subtract).then_inc(tT_lo, 1)

                def split_up(e, odd):
                    wait(dve, up_hi, e, 1, 1)
                    dve.tensor_tensor(w_lo[odd][:, 0:2, :], w_raw[odd][:, 0:2, :],
                                      w_hi[odd][:, 0:2, :].bitcast(F32), ALU.subtract).then_inc(up_split, 1)

                def split_down(e, odd):
                    wait(dve, down_hi, e, 1, 1)
                    dve.tensor_tensor(w_lo[odd][:, 2, :], w_raw[odd][:, 2, :], w_hi[odd][:, 2, :].bitcast(F32),
                                      ALU.subtract).then_inc(down_split, 1)

                dve.wait_ge(l_ready, 1)
                dve.wait_ge(e_consts, NE + 1)
                wide = [128, TT, NE]
                falling = order16[:, :].unsqueeze(1).to_broadcast(wide)
                link(dve.tensor_copy(logits[:, :, :], bank(4, width=TT * NE, a=TT)))
                for n in range(2):
                    link(dve.tensor_reduce(top[:, n, :], logits[:, :, :], AX.X, ALU.max))
                    link(dve.tensor_tensor(rank[:, :, :], logits[:, :, :],
                                           top[:, n, :].unsqueeze(2).to_broadcast(wide), ALU.is_equal))
                    link(dve.tensor_tensor(rank[:, :, :], rank[:, :, :], falling, ALU.mult))
                    link(dve.tensor_reduce(top[:, 4, :], rank[:, :, :], AX.X, ALU.max))
                    link(dve.tensor_tensor(pick[n][:, :, :], rank[:, :, :],
                                           top[:, 4, :].unsqueeze(2).to_broadcast(wide), ALU.is_equal))
                    if n == 0:
                        link(dve.scalar_tensor_tensor(logits[:, :, :].rearrange("p t e -> p (t e)"),
                                                      pick[0][:, :, :].rearrange("p t e -> p (t e)"), -3e38,
                                                      logits[:, :, :].rearrange("p t e -> p (t e)"),
                                                      ALU.mult, ALU.add))
                dve.tensor_tensor(top[:, 2, :], top[:, 1, :], top[:, 0, :], ALU.subtract).then_inc(g_diff, 1)
                split_up(0, 0)
                dve.wait_ge(g_exp, 1)
                link(dve.tensor_scalar(top[:, 4, :], top[:, 3, :], 1.0, None, ALU.add))
                link(dve.reciprocal(top[:, 5, :], top[:, 4, :]))
                link(dve.tensor_tensor(pick[1][:, :, :], pick[1][:, :, :],
                                       top[:, 3, :].unsqueeze(2).to_broadcast(wide), ALU.mult))
                link(dve.tensor_tensor(pick[0][:, :, :], pick[0][:, :, :], pick[1][:, :, :], ALU.add))
                dve.tensor_tensor(gates[:, :, 0:NE], pick[0][:, :, :],
                                  top[:, 5, :].unsqueeze(2).to_broadcast(wide), ALU.mult).then_inc(g_done, 1)
                dve.memset(yT[:, NTOK:TPAD], 0.0).then_inc(out_copied, 1)
                dve.wait_ge(b_copied, 1)

                def emit(e, odd):
                    for n in range(NU):
                        if behind(e, odd, n):
                            be, bodd, bn = behind(e, odd, n)
                            m, c = UNITS[bn]
                            cs = slice(c * CT, (c + 1) * CT)
                            wait(dve, hhi_done, be, NU, bn + 1)
                            dve.tensor_tensor(h_lo[bodd][:, m, cs], gated[:, bn % 4, :],
                                              h_hi[bodd][:, m, cs].bitcast(F32), ALU.subtract).then_inc(hlo_done, 1)
                        if known(e) and e == NX:
                            continue
                        m, c = UNITS[n]
                        wait(dve, silu_done, e, NU, n + 1)
                        wait(dve, gated_done, e, NU, n - 1)
                        j = 2 * e + m
                        bias = b_cols[:, 1, j:j + 1] if known(e) else b_cols[:, 1, bass.ds(j, 1)]
                        dve.scalar_tensor_tensor(hid[n % 2][:, :], bank(2 * (n % 2) + 1, width=CT), bias,
                                                 act_out[n % 2][:, :], ALU.add, ALU.mult).then_inc(hid_done, 1)
                        if n == 3:
                            split_down(e, odd)
                        if n == 6 and not (known(e) and e + 1 >= NX):
                            split_up(e + 1, 1 - odd)

                turns(dve, emit)
                for g in range(1, NTG, 2):
                    dve.wait_ge(out_done, (NX - 1) * NTG + g + 1)
                    dve.tensor_copy(yT[:, g * CT:(g + 1) * CT], bank(4 + g, width=CT)).then_inc(out_copied, 1)
                for g in range(NTG):
                    ts, n = TG[g], ntiles(g)
                    dve.wait_ge(y_turned, g + 1)
                    dve.tensor_tensor(y[:, ts, :], bank(g, width=128 * n, a=n), y[:, ts, :], ALU.add)\
                        .then_inc(y_added, 1)

            @block.tensor
            def _(pe):
                for g in range(NTG):
                    pe.wait_ge(e_normed, g + 1)
                    for i in range(ntiles(g)):
                        last = pe.transpose(bank(g)[:, i * 128:(i + 1) * 128], nrm3[:, TG[g].start + i, :], ident[:, :])
                    last.then_inc(tT_ready, 1)
                pe.wait_ge(e_small_in, 16 * 7)
                for n in range(2):
                    last = pe.transpose(bank(7)[:, n * 2 * NX:(n + 1) * 2 * NX], b_rows[:, n, :],
                                        ident[0:2 * NX, 0:2 * NX])
                last.then_inc(b_ready, 1)
                pe.wait_ge(wg_split, 1)
                for g in range(NTG):
                    pe.wait_ge(tT_lo, g + 1)
                    for t in range(TG[g].start, TG[g].stop):
                        dst = bank(4)[:, t * NE:(t + 1) * NE]
                        cs = slice(t * 128, (t + 1) * 128)
                        pe.matmul(dst, t_hi[:, cs], wg_hi[:, :], start=True, stop=False)
                        pe.matmul(dst, t_hi[:, cs], wg_lo[:, :], start=False, stop=False)
                        last = pe.matmul(dst, t_lo[:, cs], wg_hi[:, :], start=False, stop=True)
                last.then_inc(l_ready, 1)
                pe.wait_ge(g_done, 1)
                for g in range(NTG):
                    for i in range(ntiles(g)):
                        last = pe.transpose(bank(g, NX)[:, i * 128:(i + 1) * 128],
                                            gates[:, TG[g].start + i, :], ident[:, :])
                    last.then_inc(gT_ready, 1)
                pe.wait_ge(b_copied, 1)
                pe.wait_ge(gT_copied, NTG)
                for c in range(NTG):
                    pe.matmul(bank(4 + c, width=CT), b2_rows[:, :], gatesT[0:NE + 1, c * CT:(c + 1) * CT],
                              start=True, stop=False)

                def emit(e, odd):
                    def unit(n):
                        m, c = UNITS[n]
                        if n == 0:
                            wait(pe, up_split, e, 1, 1)
                        wait(pe, silu_done, e, NU, n - 1)
                        wait(pe, hid_done, e, NU, n - 1)
                        ts, ms = slice(c * CT, (c + 1) * CT), slice(m * 128, (m + 1) * 128)
                        for k in range(2):
                            dst = bank(2 * (n % 2) + k, width=CT)
                            pe.matmul(dst, w_hi[odd][:, k, ms], t_hi[:, ts], start=True, stop=False)
                            pe.matmul(dst, w_hi[odd][:, k, ms], t_lo[:, ts], start=False, stop=False)
                            last = pe.matmul(dst, w_lo[odd][:, k, ms], t_hi[:, ts], start=False, stop=True)
                        last.then_inc(ab_ready, 1)

                    def down(c):
                        prev, p = e - 1, 1 - odd
                        if c == 0:
                            wait(pe, down_split, prev, 1, 1)
                        wait(pe, hlo_done, prev, NU, 2 * c + 2)
                        dst, cs = bank(4 + c, width=CT), slice(c * CT, (c + 1) * CT)
                        for m in range(2):
                            w = slice(m * D, (m + 1) * D)
                            pe.matmul(dst, w_hi[p][:, 2, w], h_hi[p][:, m, cs], start=False, stop=False)
                            pe.matmul(dst, w_hi[p][:, 2, w], h_lo[p][:, m, cs], start=False, stop=False)
                            last = pe.matmul(dst, w_lo[p][:, 2, w], h_hi[p][:, m, cs], start=False,
                                             stop=(known(e) and e == NX and m == 1))
                        last.then_inc(out_done, 1)

                    for n in range(NU):
                        if not (known(e) and e == NX):
                            unit(n)
                        if n % 2 and not (known(e) and e == 0):
                            down(n // 2)

                turns(pe, emit)
                pe.wait_ge(out_copied, NTG + 1)
                for g in range(NTG):
                    for i in range(ntiles(g)):
                        t = TG[g].start + i
                        last = pe.transpose(bank(g)[:, i * 128:(i + 1) * 128], yT[:, t * 128:(t + 1) * 128],
                                            ident[:, :])
                    last.then_inc(y_turned, 1)


_INS = ["x", "ctx_1024", "mask_BxSxS2_bk1", "L0_attn_WQ", "L0_attn_WK", "L0_attn_WV",
        "L0_xattn_W_Q", "L0_xattn_b_Q", "L0_xattn_W_K", "L0_xattn_b_K", "L0_xattn_W_V", "L0_xattn_b_V",
        "L0_xattn_W_out", "L0_xattn_b_out",
        "L0_ffn_Wg", "L0_ffn_W1", "L0_ffn_b1", "L0_ffn_W11", "L0_ffn_b11", "L0_ffn_W2", "L0_ffn_b2",
        "L0_ffn_Ws1", "L0_ffn_bs1", "L0_ffn_Ws11", "L0_ffn_bs11", "L0_ffn_Ws2", "L0_ffn_bs2"]


def kernel(**inputs):
    import numpy as _np
    import concourse.bacc as _bacc
    from concourse import mybir as _mybir
    from concourse.bass_utils import run_bass_kernel_spmd as _run

    nc = _bacc.Bacc("TRN2", target_bir_lowering=False, num_devices=1)
    arrays, args = {}, []
    for name in _INS:
        a = _np.ascontiguousarray(inputs[name])
        arrays[f"in_{name}"] = a
        args.append(nc.dram_tensor(f"in_{name}", a.shape, _mybir.dt.from_np(a.dtype), kind="ExternalInput").ap())
    res = nc.dram_tensor("out_0", (NTOK, D), F32, kind="ExternalOutput").ap()
    decoder(nc, *args, res)
    r = _run(nc, [arrays], core_ids=[0])
    return r.results[0]["out_0"].reshape(NB, S, D)
```
